# Optimizing a Trainium2 kernel written in Bass

```python
import numpy as np
import jax
import jax.numpy as jnp

def _softmax(x, axis=-1):
    return jax.nn.softmax(x, axis=axis)

def _gelu(x):
    return jax.nn.gelu(x, approximate=True)

def _silu(x):
    return jax.nn.silu(x)

def _sigmoid(x):
    return jax.nn.sigmoid(x)

def _layernorm(x, axis=-1, eps=1e-05):
    m = jnp.mean(x, axis=axis, keepdims=True)
    v = jnp.var(x, axis=axis, keepdims=True)
    return (x - m) / jnp.sqrt(v + eps)

def _scatter_add(tgt, idx, src, axis=0):
    return tgt.at[idx].add(src)

def _segment_sum(src, seg, n):
    return jax.ops.segment_sum(src, seg, n)
kernel_name = 'mk_metaformer_d1_conv_nchw512_r4_4e329b'

def setup_inputs(seed: int=0):
    np.random.seed(seed)
    _w = jnp.asarray

    def _rec_inputs():
        import jax
        import jax.numpy as jnp
        _gk = jax.random.key(seed)
        x = -0.000125 + 0.9999 * jax.random.normal(jax.random.fold_in(_gk, 1), (4, 128, 32, 32), jnp.float32)
        return x
    x = _rec_inputs()

    def _L0_conv_setup():
        import jax, jax.numpy as jnp
        import numpy as np
        CH = 128
        CI = CH // 4
        DILS = (1, 4, 8, 12)
        GN_GROUPS = 32

        def conv2d(x, w, dil=1, pad=0):
            return jax.lax.conv_general_dilated(x, w, window_strides=(1, 1), padding=[(pad, pad), (pad, pad)], rhs_dilation=(dil, dil), dimension_numbers=('NCHW', 'OIHW', 'NCHW'))

        def group_norm(x, gamma, beta, groups=GN_GROUPS, eps=1e-05):
            N, C, H, W = x.shape
            xg = x.reshape(N, groups, C // groups, H, W)
            mu = jnp.mean(xg, axis=(2, 3, 4), keepdims=True)
            var = jnp.var(xg, axis=(2, 3, 4), keepdims=True)
            xn = ((xg - mu) * jax.lax.rsqrt(var + eps)).reshape(N, C, H, W)
            return xn * gamma[None, :, None, None] + beta[None, :, None, None]

        def dyn_branch(xd, w_cat, d):
            f = jax.nn.softmax(conv2d(xd, w_cat, dil=d, pad=d), axis=1)
            N, C, H, W = xd.shape
            xp = jnp.pad(xd, ((0, 0), (0, 0), (d, d), (d, d)))
            out = jnp.zeros_like(xd)
            k = 0
            for i in range(3):
                for j in range(3):
                    out = out + xp[:, :, i * d:i * d + H, j * d:j * d + W] * f[:, k:k + 1]
                    k += 1
            return out
        key = jax.random.key(seed)
        ks = jax.random.split(key, 16)
        s = 0.05
        return {'x': jax.random.normal(ks[0], (4, CH, 32, 32), jnp.float32), 'w_scale1': jax.random.normal(ks[1], (CI, CH, 1, 1), jnp.float32) * s, 'gn1_g': jnp.ones((CI,), jnp.float32), 'gn1_b': jnp.zeros((CI,), jnp.float32), 'w_cata': jax.random.normal(ks[2], (9, CI, 3, 3), jnp.float32) * s, 'w_catb': jax.random.normal(ks[3], (9, CI, 3, 3), jnp.float32) * s, 'w_catc': jax.random.normal(ks[4], (9, CI, 3, 3), jnp.float32) * s, 'w_catd': jax.random.normal(ks[5], (9, CI, 3, 3), jnp.float32) * s, 'w_scale2': jax.random.normal(ks[6], (CI, 5 * CI, 1, 1), jnp.float32) * s, 'gn2_g': jnp.ones((CI,), jnp.float32), 'gn2_b': jnp.zeros((CI,), jnp.float32), 'w_scale3': jax.random.normal(ks[7], (CH, CI, 1, 1), jnp.float32) * s, 'gn3_g': jnp.ones((CH,), jnp.float32), 'gn3_b': jnp.zeros((CH,), jnp.float32)}
    _L0_conv_all = _L0_conv_setup()
    _L0_conv_in = {k: v for k, v in _L0_conv_all.items() if k in ('w_scale1', 'gn1_g', 'gn1_b', 'w_cata', 'w_catb', 'w_catc', 'w_catd', 'w_scale2', 'gn2_g', 'gn2_b', 'w_scale3', 'gn3_g', 'gn3_b')}
    del _L0_conv_all

    def _L0_ffn_setup():
        import jax, jax.numpy as jnp
        import numpy as np
        B, S, D = (8, 512, 128)
        E, K, H = (8, 2, 512)
        key = jax.random.key(seed)
        ks = jax.random.split(key, 6)
        scale = 0.02
        return {'x': jax.random.normal(ks[0], (B, S, D), dtype=jnp.float32), 'gate_w': jax.random.normal(ks[1], (E, D), dtype=jnp.float32) * scale, 'w1': jax.random.normal(ks[2], (E, H, D), dtype=jnp.float32) * scale, 'b1': jax.random.normal(ks[3], (E, H), dtype=jnp.float32) * scale, 'w2': jax.random.normal(ks[4], (E, D, H), dtype=jnp.float32) * scale, 'b2': jax.random.normal(ks[5], (E, D), dtype=jnp.float32) * scale}
    _L0_ffn_all = _L0_ffn_setup()
    _L0_ffn_in = {k: v for k, v in _L0_ffn_all.items() if k in ('gate_w', 'w1', 'b1', 'w2', 'b2')}
    del _L0_ffn_all
    return {'x': x, 'L0_conv_w_scale1': _L0_conv_in['w_scale1'], 'L0_conv_gn1_g': _L0_conv_in['gn1_g'], 'L0_conv_gn1_b': _L0_conv_in['gn1_b'], 'L0_conv_w_cata': _L0_conv_in['w_cata'], 'L0_conv_w_catb': _L0_conv_in['w_catb'], 'L0_conv_w_catc': _L0_conv_in['w_catc'], 'L0_conv_w_catd': _L0_conv_in['w_catd'], 'L0_conv_w_scale2': _L0_conv_in['w_scale2'], 'L0_conv_gn2_g': _L0_conv_in['gn2_g'], 'L0_conv_gn2_b': _L0_conv_in['gn2_b'], 'L0_conv_w_scale3': _L0_conv_in['w_scale3'], 'L0_conv_gn3_g': _L0_conv_in['gn3_g'], 'L0_conv_gn3_b': _L0_conv_in['gn3_b'], 'L0_ffn_gate_w': _L0_ffn_in['gate_w'], 'L0_ffn_w1': _L0_ffn_in['w1'], 'L0_ffn_b1': _L0_ffn_in['b1'], 'L0_ffn_w2': _L0_ffn_in['w2'], 'L0_ffn_b2': _L0_ffn_in['b2']}

def reference(x, L0_conv_w_scale1, L0_conv_gn1_g, L0_conv_gn1_b, L0_conv_w_cata, L0_conv_w_catb, L0_conv_w_catc, L0_conv_w_catd, L0_conv_w_scale2, L0_conv_gn2_g, L0_conv_gn2_b, L0_conv_w_scale3, L0_conv_gn3_g, L0_conv_gn3_b, L0_ffn_gate_w, L0_ffn_w1, L0_ffn_b1, L0_ffn_w2, L0_ffn_b2):
    import jax
    import jax.numpy as jnp

    def _L0_conv_ref(x, w_scale1, gn1_g, gn1_b, w_cata, w_catb, w_catc, w_catd, w_scale2, gn2_g, gn2_b, w_scale3, gn3_g, gn3_b):
        import jax, jax.numpy as jnp
        import numpy as np
        CH = 128
        CI = CH // 4
        DILS = (1, 4, 8, 12)
        GN_GROUPS = 32

        def conv2d(x, w, dil=1, pad=0):
            return jax.lax.conv_general_dilated(x, w, window_strides=(1, 1), padding=[(pad, pad), (pad, pad)], rhs_dilation=(dil, dil), dimension_numbers=('NCHW', 'OIHW', 'NCHW'))

        def group_norm(x, gamma, beta, groups=GN_GROUPS, eps=1e-05):
            N, C, H, W = x.shape
            xg = x.reshape(N, groups, C // groups, H, W)
            mu = jnp.mean(xg, axis=(2, 3, 4), keepdims=True)
            var = jnp.var(xg, axis=(2, 3, 4), keepdims=True)
            xn = ((xg - mu) * jax.lax.rsqrt(var + eps)).reshape(N, C, H, W)
            return xn * gamma[None, :, None, None] + beta[None, :, None, None]

        def dyn_branch(xd, w_cat, d):
            f = jax.nn.softmax(conv2d(xd, w_cat, dil=d, pad=d), axis=1)
            N, C, H, W = xd.shape
            xp = jnp.pad(xd, ((0, 0), (0, 0), (d, d), (d, d)))
            out = jnp.zeros_like(xd)
            k = 0
            for i in range(3):
                for j in range(3):
                    out = out + xp[:, :, i * d:i * d + H, j * d:j * d + W] * f[:, k:k + 1]
                    k += 1
            return out
        xd = jax.nn.relu(group_norm(conv2d(x, w_scale1), gn1_g, gn1_b))
        outs = [dyn_branch(xd, w, d) for w, d in zip((w_cata, w_catb, w_catc, w_catd), DILS)]
        cat = jnp.concatenate([xd] + outs, axis=1)
        y = jax.nn.relu(group_norm(conv2d(cat, w_scale2), gn2_g, gn2_b))
        y = jax.nn.relu(group_norm(conv2d(y, w_scale3), gn3_g, gn3_b))
        return y

    def _L0_ffn_ref(x, gate_w, w1, b1, w2, b2):
        import jax, jax.numpy as jnp
        import numpy as np
        B, S, D = (8, 512, 128)
        E, K, H = (8, 2, 512)
        batch, seq, dim = x.shape
        x_flat = x.reshape(-1, dim)
        T = x_flat.shape[0]
        gate_logits = x_flat @ gate_w.T
        topk_vals, topk_idx = jax.lax.top_k(gate_logits, K)
        topk_w = jax.nn.softmax(topk_vals, axis=-1)
        comb = jnp.zeros((T, E), dtype=x_flat.dtype)
        comb = comb.at[jnp.arange(T)[:, None], topk_idx].add(topk_w)
        out = jnp.zeros_like(x_flat)
        for e in range(E):
            h = jax.nn.gelu(x_flat @ w1[e].T + b1[e], approximate=False)
            y = h @ w2[e].T + b2[e]
            out = out + comb[:, e:e + 1] * y
        return out.reshape(batch, seq, dim)

    def _gn(v, G=32, eps=1e-05):
        B_, C_, H_, W_ = v.shape
        g = v.reshape(B_, G, C_ // G, H_, W_)
        m = jnp.mean(g, axis=(2, 3, 4), keepdims=True)
        s = jnp.var(g, axis=(2, 3, 4), keepdims=True)
        return ((g - m) / jnp.sqrt(s + eps)).reshape(v.shape)

    def _ln_c(v, eps=1e-06):
        m = jnp.mean(v, axis=1, keepdims=True)
        s = jnp.var(v, axis=1, keepdims=True)
        return (v - m) / jnp.sqrt(s + eps)

    def _ln_t(v, eps=1e-05):
        m = jnp.mean(v, axis=-1, keepdims=True)
        s = jnp.var(v, axis=-1, keepdims=True)
        return (v - m) / jnp.sqrt(s + eps)

    def _to_tokens(v):
        B_, C_, H_, W_ = v.shape
        return v.reshape(B_, C_, H_ * W_).transpose(0, 2, 1)

    def _from_tokens(t, like):
        B_, C_, H_, W_ = like.shape
        return t.transpose(0, 2, 1).reshape(B_, C_, H_, W_)
    x = x + _L0_conv_ref(_ln_c(x), L0_conv_w_scale1, L0_conv_gn1_g, L0_conv_gn1_b, L0_conv_w_cata, L0_conv_w_catb, L0_conv_w_catc, L0_conv_w_catd, L0_conv_w_scale2, L0_conv_gn2_g, L0_conv_gn2_b, L0_conv_w_scale3, L0_conv_gn3_g, L0_conv_gn3_b)
    t = _to_tokens(x)
    t = t + _L0_ffn_ref(_ln_t(t), L0_ffn_gate_w, L0_ffn_w1, L0_ffn_b1, L0_ffn_w2, L0_ffn_b2)
    x = _from_tokens(t, x)
    return x

_drawn_inputs = setup_inputs


def setup_inputs(seed=0):
    import zlib

    import numpy as np

    out = dict(_drawn_inputs(seed))
    spreads = {'L0_conv_gn1_g': (1.0, 0.2),
     'L0_conv_gn1_b': (0.0, 0.1),
     'L0_conv_gn2_g': (1.0, 0.2),
     'L0_conv_gn2_b': (0.0, 0.1),
     'L0_conv_gn3_g': (1.0, 0.2),
     'L0_conv_gn3_b': (0.0, 0.1)}
    factors = {'L0_ffn_b1': 8.0, 'L0_ffn_b2': 4.854}
    for name, (base, spread) in spreads.items():
        noise = np.random.default_rng([zlib.crc32(name.encode()), seed]).standard_normal(out[name].shape)
        drawn = base * np.exp(spread * noise) if base else spread * noise
        out[name] = jnp.asarray(drawn.astype(out[name].dtype))
    for name, factor in factors.items():
        out[name] = (out[name] * factor).astype(out[name].dtype)
    return out
```

```python
from contextlib import ExitStack

import concourse.bass as bass
import numpy as np
from concourse import mybir
from concourse.alu_op_type import AluOpType as ALU

ACT = mybir.ActivationFunctionType
F32 = mybir.dt.float32
F16 = mybir.dt.float16
I32 = mybir.dt.int32
U32 = mybir.dt.uint32
AX_X = mybir.AxisListType.X

P = 128
B, C, HH, WW = 4, 128, 32, 32
HW = HH * WW
T = B * HW
CI = 32
KK = 9
DILS = (1, 4, 8, 12)
ND = len(DILS)
PAD = max(DILS)
WP = HH + 2 * PAD
HALF = HW // 2
RH = HH // 2
PT = HW // P
TT = T // P
E, HID = 8, 512
HC = HID // P
NQ = (2 * T + E * (P - 1)) // P
LN_C_EPS, GN_EPS, LN_T_EPS = 1e-6, 1e-5, 1e-5

SX = 2.0 ** 7
SW = 2.0 ** 8
SF = 2.0 ** 12
SN = 2.0 ** 11
SH = 2.0 ** 6

COLS = {}


def _cols():
    at = 0
    for name, n in (("gn", 6), ("b1", E * HC), ("w1", CI), ("gate", E), ("wcat", KK * ND * KK), ("w2", 5 * CI),
                    ("w3", C), ("ident", P), ("avg", P), ("group", P), ("fold", 4 * KK), ("iota8", E),
                    ("iotaq", NQ), ("row1", 1)):
        COLS[name] = (at, at + n)
        at += n
    return at


NS = _cols()
C16 = {"ident": (0, P), "before": (P, 2 * P), "ones": (2 * P, 3 * P), "iota": (3 * P, 4 * P),
       "iotaq": (4 * P, 4 * P + NQ), "sel": (4 * P + NQ, 4 * P + NQ + KK * P)}
NC16 = C16["sel"][1]


def shape_constants():
    c32 = np.zeros((P, NS - COLS["ident"][0]), np.float32)
    base = COLS["ident"][0]

    def put(name, value, rows=P):
        a, b = COLS[name]
        c32[:rows, a - base:b - base] = value

    put("ident", np.eye(P))
    put("avg", 1.0 / C)
    put("group", np.kron(np.eye(C // 4), np.full((4, 4), 0.25)))
    put("fold", np.concatenate([np.eye(4 * KK), np.eye(4 * KK)]), 8 * KK)
    put("iota8", np.arange(E))
    put("iotaq", np.arange(NQ))
    put("row1", np.arange(1, P + 1)[:, None])
    c16 = np.zeros((P, NC16), np.float16)
    c16[:, 0:P] = np.eye(P)
    c16[:, P:2 * P] = np.triu(np.ones((P, P)), 1)
    c16[:, 2 * P:3 * P] = 1.0
    c16[:, 3 * P:4 * P] = np.arange(P)
    c16[:, 4 * P:4 * P + NQ] = np.arange(NQ)
    sel = np.zeros((B, KK, 2, KK, B, CI), np.float16)
    for b in range(B):
        for k in range(KK):
            sel[b, k, :, k, b, :] = 1.0
    c16[:B * KK * 2, 4 * P + NQ:] = sel.reshape(B * KK * 2, KK * P)
    return c32, c16


def build(nc, x, small, c16, w1t, w2t, b2, out):
    ctx = ExitStack()
    with ctx:
        def sb(name, shape, dt=F32):
            return ctx.enter_context(nc.sbuf_tensor(name, shape, dt))

        def sem(name):
            return ctx.enter_context(nc.semaphore(name))

        X = sb("X", [P, T])
        prm = sb("prm", [P, NS])
        k16 = sb("k16", [P, NC16], F16)
        WST = sb("WST", [P, 2, E * HID])
        W1S = sb("W1S", [P, E, 2, HID], F16)
        W2S = sb("W2S", [P, E, 2, HID], F16)
        B2 = sb("B2", [P, E * C])
        RG = sb("RG", [P, P + E])
        WC1 = sb("WC1", [P, CI])
        WCS = sb("WCS", [P, 2, KK * ND * KK], F16)
        WCB = sb("WCB", [P, KK, ND, 8 * KK], F16)
        W2B = sb("W2B", [P, 5, P])
        W3Z = sb("W3Z", [P, B, P])
        MV = sb("MV", [P, 2 * HW])
        MSQ, VAR = MV[:, 0:HW], MV[:, HW:2 * HW]
        XHL = MV[:, :].bitcast(F16).rearrange("p (s i n) -> p s i n", s=2, i=PT)
        Z = sb("Z", [P, HW])
        RX = sb("RX", [P, 2 * WP * WP])
        XD = RX[:, 0:WP * WP].rearrange("p (h w) -> p h w", w=WP)
        XH = RX[:, WP * WP:3 * WP * WP // 2].bitcast(F16).rearrange("p (h w) -> p h w", w=WP)
        XL = RX[:, 3 * WP * WP // 2:2 * WP * WP].bitcast(F16).rearrange("p (h w) -> p h w", w=WP)
        XTL = RX[:, 0:TT * (C + E)].rearrange("p (t n) -> p t n", t=TT)
        st = sb("st", [P, 2, 6])
        aff = sb("aff", [P, 16])
        LOG = sb("LOG", [P, ND, HW])
        R3 = LOG[:, 0:2, :]
        XN = LOG[:, 2:4, :].rearrange("p s (i n) -> p s i n", n=C)
        FE = sb("FE", [P, 2, PT * B * KK])
        mx = sb("mx", [P, ND, PT * B])
        FHL = sb("FHL", [P, ND, PT * B * KK, 2], F16)
        FT = sb("FT", [P, ND, HW], F16)
        NP_ = 6
        PR = sb("PR", [P, NP_, HW])
        XSQ = PR[:, 0:T // HW, :].rearrange("p a n -> p (a n)")
        Y2 = Z
        OHR = WST[:, 0, :].bitcast(F16).rearrange("p (n r) -> p n r", r=P)
        OHQ = PR[:, :, :].rearrange("p a n -> p (a n)")[:, 0:2 * TT * NQ].bitcast(F16).rearrange(
            "p (n v q) -> p n v q", v=2, q=NQ)
        YIN = WST[:, :, :].rearrange("p j (t c) -> p j t c", c=C)
        CMB = PR[:, 0:2, :].rearrange("p s (i n) -> p s i n", n=C)
        OUT = PR[:, 2:4, :]
        st3 = sb("st3", [P, B, 2, 6])
        mv3 = sb("mv3", [P, B, 10])
        st4 = sb("st4", [P, TT, 6])
        ts = sb("ts", [P, 5, TT])
        rN, nb = ts[:, 3, :], ts[:, 4, :]
        gw = sb("gw", [P, 12, TT])
        g8 = FT[:, :, :].rearrange("p d n -> p (d n)").bitcast(F32).rearrange("p (k n) -> p k n", k=8)
        mask16 = sb("mask16", [P, E * TT], F16)
        e8 = sb("e8", [P, 8, E])
        e8i = sb("e8i", [P, 2, E], I32)
        si = sb("si", [P, 3, 2 * TT], I32)
        qr = sb("qr", [P, 2, 2 * TT])
        ge = FHL[:, :, :, :].rearrange("p d g v -> p (d g v)").bitcast(F32)[:, 0:NQ * E]
        eid = sb("eid", [P, NQ])
        eidi = sb("eidi", [P, NQ], I32)
        dst = sb("dst", [P, 3, NQ])
        dsti = sb("dsti", [P, 3, NQ], I32)
        NR = 4
        gidx, sidx = sb("gidx", [P, NR], I32), sb("sidx", [P, NR], I32)
        GX = sb("GX", [P, NR, 2 * C], F16)
        XT = sb("XT", [P, 2, 2 * C], F16)
        GF = WCB[:, :, :, :].rearrange("p t d m -> p (t d m)").bitcast(F32)[:, 0:2 * HID].rearrange("p (s n) -> p s n", s=2)
        HS = RX[:, TT * (C + E):TT * (C + E) + 2 * HID].bitcast(F16).rearrange("p (s v n) -> p s v n", s=2, v=2)
        YH = sb("YH", [P, 2, C])
        YS = W3Z
        PS = ctx.enter_context(nc.psum_tensor("PS", [P, 8, 512], F32))

        xr = nc.dram_tensor("token_rows", [T, 2 * C], F16).ap()
        yr = nc.dram_tensor("expert_rows", [2 * T, C], F32).ap()

        def prm_(name):
            a, b = COLS[name]
            return prm[:, a:b]

        def k16_(name):
            a, b = C16[name]
            return k16[:, a:b]

        def bank(i, n=512):
            return PS[:, i, 0:n]

        def banks2(i):
            return PS[:, i:i + 2, :].rearrange("p a n -> p (a n)")

        def tap_view(t, d, k, r0=0, rows=HH):
            oy, ox = PAD + d * (k // 3 - 1) + r0, PAD + d * (k % 3 - 1)
            return t[:, oy:oy + rows, ox:ox + WW]

        def plane(v):
            return v.rearrange("p (h w) -> p h w", w=WW)

        small_in, c16_in, w_in, b2_in = sem("small_in"), sem("c16_in"), sem("w_in"), sem("b2_in")
        x_in = [sem(f"x_in{b}") for b in range(B)]
        wmean_done = sem("wmean_done")
        wc_ready = sem("wc_ready")
        wcb_ready, w2b_ready, w3z_ready = sem("wcb_ready"), sem("w2b_ready"), sem("w3z_ready")
        zero_done = sem("zero_done")
        xsq_done = sem("xsq_done")
        mean_done, u_done, msq_done = sem("mean_done"), sem("u_done"), sem("msq_done")
        mean2_done, var_done, std_done = sem("mean2_done"), sem("var_done"), sem("std_done")
        gvar_done, gstd_done, gaff_done = sem("gvar_done"), sem("gstd_done"), sem("gaff_done")
        xd_done, xh_done, xl_done = sem("xd_done"), sem("xh_done"), sem("xl_done")
        logit_done, log_done, tlog_done = sem("logit_done"), sem("log_done"), sem("tlog_done")
        fsub_done, fexp_done, fhl_done = sem("fsub_done"), sem("fexp_done"), sem("fhl_done")
        ft_done, ftc_done = sem("ft_done"), sem("ftc_done")
        fb_done, prod_done, pair_done, acc_done = sem("fb_done"), sem("prod_done"), sem("pair_done"), sem("acc_done")
        gn2v_done, gn2s_done, gn2a_done, y2_done = sem("gn2v_done"), sem("gn2s_done"), sem("gn2a_done"), sem("y2_done")
        y3_done, gs_done, gm_done = sem("y3_done"), sem("gs_done"), sem("gm_done")
        gn3v_done, gn3s_done, gn3a_done = sem("gn3v_done"), sem("gn3s_done"), sem("gn3a_done")
        r3_done, x1_done = sem("r3_done"), sem("x1_done")
        tok_done, tokc_done = sem("tok_done"), sem("tokc_done")
        tvar_done, tstd_done, taff_done = sem("tvar_done"), sem("tstd_done"), sem("taff_done")
        xn_done, hi_done, lo_done, rows_out = sem("xn_done"), sem("hi_done"), sem("lo_done"), [sem(f"rows_out{b}") for b in range(B)]
        gsub_done, gexp_done = sem("gsub_done"), sem("gexp_done")
        mask_done, rank_done = sem("mask_done"), sem("rank_done")
        qr_done, ohr_done, ohq_done, row_ready = sem("qr_done"), sem("ohr_done"), sem("ohq_done"), sem("row_ready")
        dest_done, eid_done = sem("dest_done"), sem("eid_done")
        whi_done, wlo_done, b2_ready = sem("whi_done"), sem("wlo_done"), sem("b2_ready")
        gidx_ready = sem("gidx_ready")
        g_in = [sem(f"g_in{j}") for j in range(4)]
        y_out = [sem(f"y_out{j}") for j in range(4)]
        xt_done, xtc_done, h_done, gelu_done = sem("xt_done"), sem("xtc_done"), sem("h_done"), sem("gelu_done")
        split_done, y_done, ys_done = sem("split_done"), sem("y_done"), sem("ys_done")
        y_in = [sem(f"y_in{b}") for b in range(B)]
        first_done, comb_done, ot_done, fin_done = sem("first_done"), sem("comb_done"), sem("ot_done"), sem("fin_done")
        gates_done = sem("gates_done")
        hs_done, yh_done = sem("hs_done"), sem("yh_done")
        dve_step, act_step, pool_step = sem("dve_step"), sem("act_step"), sem("pool_step")
        out_done = [sem(f"out_done{b}") for b in range(B)]
        pool_held = sem("pool_held")

        products = [(d, k) for d in range(ND) for k in range(KK)]
        units = []
        for d in range(ND):
            for k in range(0, KK - 1, 2):
                units.append((d, d * KK + k, d * KK + k + 1))
            units.append((d, d * KK + KK - 1, d * KK + KK - 1))
        LAG = 3

        def unit_of(n):
            for i, (_, first, last) in enumerate(units):
                if first <= n <= last:
                    return i

        def pairs_before(n):
            return sum(1 for _, first, last in units if last > first and last <= n)

        def weight_split(w, half):
            n = (HID, C)[w]
            src = WST[:, w, :].rearrange("p (g n) -> p g n", n=n)
            dest = (W1S, W2S)[w][:, :, :, :].rearrange("p e v n -> p (e v n)").rearrange("p (g v n) -> p g v n", v=2, n=n)
            g = src.shape[1] // 2
            s = slice(half * g, (half + 1) * g)
            return src[:, s, :], dest[:, s, 0, :], dest[:, s, 1, :]

        NSTEP = NQ + 1

        def run_steps(engine, step):
            laps = (NSTEP - 1) // NR
            for s in range(2 * NR):
                step(s // NR, s % NR)
            with engine.Fori(2, laps) as i:
                for j in range(NR):
                    step(i, j)
            for s in range(NR * laps, NSTEP):
                step(s // NR, s % NR)

        def tile(i, j, ahead=0):
            return NR * i + (j + ahead), (j + ahead) % NR, i + (j + ahead) // NR

        def exists(q):
            return not isinstance(q, int) or 0 <= q < NQ

        def at_least(engine, signal, value):
            if not isinstance(value, int) or value > 0:
                engine.wait_ge(signal, value)

        block = ctx.enter_context(nc.Block())

        @block.sync
        def _(sp):
            sp.dma_start(prm[:, :], small).then_inc(small_in, 16)
            for b in (1, 3):
                sp.dma_start(X[:, b * HW:(b + 1) * HW], x[b]).then_inc(x_in[b], 16)
            sp.dma_start(WST[:, 0, :], w1t).then_inc(w_in, 16)
            sp.dma_start(B2[0:1, :], b2).then_inc(b2_in, 16)
            for b in range(B):
                sp.wait_ge(hi_done, b + 1)
                sp.wait_ge(lo_done, b + 1)
                sp.dma_start(xr[b * HW:(b + 1) * HW, :].rearrange("(i p) n -> p i n", p=P),
                             XHL[:, b % 2, :, :]).then_inc(rows_out[b], 16)
            for j in range(NR):
                sp.wait_ge(y_out[j], 16 * ((NQ - 1 - j) // NR + 1))
            for b in range(B):
                for c in range(2):
                    sp.dma_start(YIN[:, c, b * PT:(b + 1) * PT, :], yr[c * T + b * HW:c * T + (b + 1) * HW, :].rearrange(
                        "(i p) n -> p i n", p=P)).then_inc(y_in[b], 16)
            for b in range(B):
                sp.wait_ge(fin_done, b + 1)
                sp.dma_start(out[b], OUT[:, b % 2, :]).then_inc(out_done[b], 16)
            for b in range(B):
                sp.wait_ge(out_done[b], 16)

        @block.gpsimd
        def _(pool):
            for t in (XD, XH, XL, WCB, W2B, W3Z):
                ap = t[:, :, :] if len(t.shape) == 3 else t[:, :, :, :].rearrange("p a b c -> p a (b c)")
                nc.gpsimd.memset(ap, 0.0).then_inc(zero_done, 1)
            pool.wait_ge(b2_in, 16)
            nc.gpsimd.partition_broadcast(B2[:, :], B2[0:1, :]).then_inc(b2_ready, 1)
            for d in range(ND):
                for k in range(1, KK - 1, 2):
                    n = d * KK + k
                    pool.wait_ge(prod_done, n + 1)
                    a, b_ = (n - 1) % NP_, n % NP_
                    nc.gpsimd.tensor_tensor(PR[:, a, :], PR[:, a, :], PR[:, b_, :], ALU.add).then_inc(pair_done, 1)
            for b in range(B):
                s = slice(b * HW, (b + 1) * HW)
                pool.wait_ge(r3_done, b + 1)
                nc.gpsimd.tensor_tensor(X[:, s], X[:, s], R3[:, b % 2, :], ALU.add).then_inc(x1_done, 1)
            pool.wait_ge(qr_done, 1)
            for n in range(2 * TT):
                nc.gpsimd.tensor_scalar(OHQ[:, n, 1, :], k16_("iotaq"), qr[:, 0, n:n + 1], float(n), ALU.is_equal,
                                        ALU.mult).then_inc(ohq_done, 1)
            for b in range(B):
                pool.wait_ge(rows_out[b], 16)

            def gather(q, slot, lap):
                pool.wait_ge(gidx_ready, q + 1)
                at_least(pool, xt_done, q - NR + 1)
                pool.sem_inc(pool_held, 1)
                nc.gpsimd.indirect_dma_start(GX[:, slot, :], None, xr, bass.IndirectOffsetOnAxis(
                    ap=gidx[:, slot:slot + 1].bitcast(U32), axis=0)).then_inc(g_in[slot], 16)

            def scatter(q, slot, lap):
                pool.wait_ge(ys_done, q + 1)
                pool.sem_inc(pool_held, 1)
                nc.gpsimd.indirect_dma_start(yr, bass.IndirectOffsetOnAxis(ap=sidx[:, slot:slot + 1].bitcast(U32), axis=0),
                                             YS[:, slot, :], None, bounds_check=2 * T - 1,
                                             oob_is_err=False).then_inc(y_out[slot], 16)

            def step(i, j):
                if exists(tile(i, j)[0]):
                    gather(*tile(i, j))
                if exists(tile(i, j, -3)[0]):
                    scatter(*tile(i, j, -3))

            run_steps(pool, step)
            for q in range(NSTEP - 3, NQ):
                scatter(q, q % NR, q // NR)

        @block.scalar
        def _(act):
            steps = [0]

            def chain(ins):
                steps[0] += 1
                ins.then_inc(act_step, 1)
                act.wait_ge(act_step, steps[0])

            for b in (0, 2):
                act.dma_start(X[:, b * HW:(b + 1) * HW], x[b]).then_inc(x_in[b], 16)
            act.dma_start(k16[:, :], c16).then_inc(c16_in, 16)
            act.dma_start(WST[:, 1, :], w2t).then_inc(w_in, 16)
            for b in range(B):
                act.wait_ge(x_in[b], 16)
                nc.scalar.activation(XSQ[:, b * HW:(b + 1) * HW], X[:, b * HW:(b + 1) * HW],
                                     ACT.Square).then_inc(xsq_done, 1)
            for h in range(2):
                act.wait_ge(mean_done, h + 1)
                nc.scalar.activation(MSQ[:, h * HALF:(h + 1) * HALF], bank(h), ACT.Square).then_inc(mean2_done, 1)
            for h in range(2):
                act.wait_ge(var_done, h + 1)
                nc.scalar.activation(MSQ[:, h * HALF:(h + 1) * HALF], VAR[:, h * HALF:(h + 1) * HALF],
                                     ACT.Sqrt).then_inc(std_done, 1)
            act.wait_ge(gvar_done, 1)
            nc.scalar.activation(aff[:, 2:3], aff[:, 1:2], ACT.Sqrt).then_inc(gstd_done, 1)
            act.wait_ge(gaff_done, 1)
            act.wait_ge(zero_done, 3)
            nc.scalar.activation(XH[:, PAD:PAD + HH, PAD:PAD + WW], plane(Z[:, :]), ACT.Relu,
                                 bias=aff[:, 7:8], scale=aff[:, 6:7]).then_inc(xh_done, 1)
            nc.scalar.activation(XD[:, PAD:PAD + HH, PAD:PAD + WW], plane(Z[:, :]), ACT.Relu,
                                 bias=aff[:, 5:6], scale=aff[:, 4:5]).then_inc(xd_done, 1)

            def evacuate_logits(d):
                act.wait_ge(logit_done, d + 1)
                for h in range(2):
                    nc.scalar.activation(LOG[0:8 * KK, d, h * HALF:(h + 1) * HALF], PS[0:8 * KK, 2 * (d % 2) + h, :],
                                         ACT.Copy, scale=1.0 / (SX * SW)).then_inc(log_done, 1)

            def exponential(d):
                act.wait_ge(fsub_done, d + 1)
                nc.scalar.activation(FE[:, d % 2, :], FE[:, d % 2, :], ACT.Exp).then_inc(fexp_done, 1)

            def evacuate_filters(d):
                act.wait_ge(ft_done, d + 1)
                nc.scalar.activation(FT[0:8 * KK, d, :], PS[0:8 * KK, 6 + d % 2, :].bitcast(F16), ACT.Copy).then_inc(ftc_done, 1)

            act.wait_ge(w_in, 32)
            for w in range(2):
                for half in range(2):
                    src, hi, _ = weight_split(w, half)
                    nc.scalar.activation(hi, src, ACT.Copy, scale=SW).then_inc(whi_done, 1)
            evacuate_logits(0)
            evacuate_logits(1)
            exponential(0)
            evacuate_logits(2)
            exponential(1)
            evacuate_filters(0)
            evacuate_logits(3)
            exponential(2)
            evacuate_filters(1)
            exponential(3)
            evacuate_filters(2)
            evacuate_filters(3)
            act.wait_ge(gn2v_done, 1)
            nc.scalar.activation(aff[:, 2:3], aff[:, 1:2], ACT.Sqrt).then_inc(gn2s_done, 1)
            act.wait_ge(gn2a_done, 1)
            nc.scalar.activation(Y2[:, :], banks2(4), ACT.Relu, bias=aff[:, 5:6], scale=aff[:, 4:5]).then_inc(y2_done, 1)
            for b in range(B + 1):
                if b < B:
                    act.wait_ge(gn3v_done, b + 1)
                    nc.scalar.activation(mv3[:, b, 5:6], mv3[:, b, 4:5], ACT.Sqrt).then_inc(gn3s_done, 1)
                    act.wait_ge(gn3a_done, b + 1)
                    if b >= 2:
                        act.wait_ge(x1_done, b - 1)
                    nc.scalar.activation(R3[:, b % 2, :], banks2(2 * (b % 2)), ACT.Relu,
                                         bias=mv3[:, b, 8:9], scale=mv3[:, b, 7:8]).then_inc(r3_done, 1)
                if b >= 1:
                    c = b - 1
                    for g in range(c * PT // 2, (c + 1) * PT // 2):
                        act.wait_ge(tok_done, g + 1)
                        nc.scalar.activation(XTL[:, 2 * g:2 * g + 2, :].rearrange("p a n -> p (a n)"),
                                             PS[:, 5 + g % 3, 0:2 * (C + E)], ACT.Copy).then_inc(tokc_done, 1)
                    act.wait_ge(tvar_done, c + 1)
                    nc.scalar.activation(ts[:, 2, c * PT:(c + 1) * PT], ts[:, 1, c * PT:(c + 1) * PT],
                                         ACT.Sqrt).then_inc(tstd_done, 1)
                    act.wait_ge(taff_done, c + 1)
                    if c >= 2:
                        act.wait_ge(lo_done, c - 1)
                        act.wait_ge(rows_out[c - 2], 16)
                    for i in range(PT):
                        t = c * PT + i
                        nc.scalar.activation(XN[:, c % 2, i, :], XTL[:, t, 0:C], ACT.Identity, bias=nb[:, t:t + 1],
                                             scale=rN[:, t:t + 1]).then_inc(xn_done, 1)
                    act.wait_ge(xn_done, PT * (c + 1))
                    nc.scalar.activation(XHL[:, c % 2, :, 0:C], XN[:, c % 2, :, :], ACT.Copy).then_inc(hi_done, 1)
            act.wait_ge(gsub_done, 1)
            nc.scalar.activation(gw[:, 3, :], gw[:, 2, :], ACT.Exp).then_inc(gexp_done, 1)
            act.wait_ge(eid_done, 1)
            b1 = prm_("b1").rearrange("p (e c) -> p e c", c=HC)

            def turned(q, slot, lap):
                act.wait_ge(xt_done, q + 1)
                at_least(act, h_done, q - 1)
                nc.scalar.activation(XT[:, slot % 2, :], PS[:, slot % 2, 0:C].bitcast(F16), ACT.Copy).then_inc(xtc_done, 1)

            def gelu(q, slot, lap):
                e = act.value_load(eidi[0:1, bass.ds(q, 1)], min_val=0, max_val=E - 1)
                act.wait_ge(h_done, q + 1)
                at_least(act, split_done, q - 1)
                for c in range(HC):
                    last = nc.scalar.activation(GF[:, slot % 2, c * P:(c + 1) * P], PS[:, 2 + slot % 2, c * P:(c + 1) * P],
                                                ACT.Gelu, bias=b1[:, bass.ds(e, 1), c], scale=1.0 / (SN * SW))
                last.then_inc(gelu_done, 1)

            turned(*tile(0, 0))

            def step(i, j):
                if exists(tile(i, j, 1)[0]):
                    turned(*tile(i, j, 1))
                if exists(tile(i, j)[0]):
                    gelu(*tile(i, j))

            run_steps(act, step)
            for t in range(TT):
                if t % PT == 0:
                    act.wait_ge(y_in[t // PT], 32)
                    if t // PT >= 2:
                        act.wait_ge(ot_done, 2 * (t // PT - 1))
                if t == 0:
                    act.wait_ge(gates_done, 1)
                nc.scalar.activation(CMB[:, (t // PT) % 2, t % PT, :], YIN[:, 0, t, :], ACT.Copy,
                                     scale=gw[:, 4, t:t + 1]).then_inc(first_done, 1)

        @block.vector
        def _(dve):
            steps = [0]

            def chain(ins):
                steps[0] += 1
                ins.then_inc(dve_step, 1)
                dve.wait_ge(dve_step, steps[0])

            dve.wait_ge(small_in, 16)
            a, g = COLS["w1"][0], COLS["gate"][0]
            nc.vector.tensor_copy(RG[:, 0:P], prm_("ident"))
            dve.wait_ge(wmean_done, 1)
            nc.vector.tensor_tensor(WC1[:, :], prm_("w1"), bank(7, CI), ALU.subtract).then_inc(wc_ready, 1)
            nc.vector.tensor_tensor(RG[:, P:P + E], prm_("gate"), PS[:, 7, CI:CI + E], ALU.subtract).then_inc(wc_ready, 1)
            chain(nc.vector.tensor_scalar(WCS[:, 0, :], prm_("wcat"), SW, None, ALU.mult))
            chain(nc.vector.scalar_tensor_tensor(WCS[:, 1, :], prm_("wcat"), SW, WCS[:, 0, :], ALU.mult, ALU.subtract))
            dve.wait_ge(zero_done, 6)
            for b in range(B):
                rows = slice(b * CI, (b + 1) * CI)
                for s in range(2):
                    o = 4 * KK * s + KK * b
                    nc.vector.tensor_copy(WCB[rows, :, :, o:o + KK], WCS[rows, s, :].rearrange(
                        "p (t d k) -> p t d k", t=KK, d=ND)).then_inc(wcb_ready, 1)
                w2 = prm_("w2").rearrange("p (s o) -> p s o", s=5)
                nc.vector.tensor_copy(W2B[rows, 0, b * CI:(b + 1) * CI], w2[rows, 0, :]).then_inc(w2b_ready, 1)
                nc.vector.tensor_scalar(W2B[rows, 1:5, b * CI:(b + 1) * CI], w2[rows, 1:5, :], 1.0 / SF, None,
                                        ALU.mult).then_inc(w2b_ready, 1)
                nc.vector.tensor_copy(W3Z[rows, b, :], prm_("w3")[rows, :]).then_inc(w3z_ready, 1)
            for h in range(2):
                s = slice(h * HALF, (h + 1) * HALF)
                dve.wait_ge(mean2_done, h + 1)
                dve.wait_ge(msq_done, h + 1)
                nc.vector.scalar_tensor_tensor(VAR[:, s], bank(4 + h), LN_C_EPS, MSQ[:, s], ALU.add,
                                               ALU.subtract).then_inc(var_done, 1)
            for h in range(2):
                s = slice(h * HALF, (h + 1) * HALF)
                dve.wait_ge(std_done, h + 1)
                chain(nc.vector.reciprocal(VAR[:, s], MSQ[:, s]))
                dve.wait_ge(u_done, h + 1)
                chain(nc.vector.tensor_tensor(Z[:, s], bank(2 + h), VAR[:, s], ALU.mult))
                chain(nc.vector.bn_stats(st[:, h, :], Z[:, s]))
            gn = prm_("gn")
            chain(nc.vector.bn_aggr(aff[:, 0:2], st[:, :, :].rearrange("p a b -> p (a b)")))
            nc.vector.tensor_scalar(aff[:, 1:2], aff[:, 1:2], GN_EPS, None, ALU.add).then_inc(gvar_done, 1)
            dve.wait_ge(gstd_done, 1)
            chain(nc.vector.reciprocal(aff[:, 3:4], aff[:, 2:3]))
            chain(nc.vector.tensor_tensor(aff[:, 4:5], aff[:, 3:4], gn[:, 0:1], ALU.mult))
            chain(nc.vector.tensor_tensor(aff[:, 5:6], aff[:, 4:5], aff[:, 0:1], ALU.mult))
            chain(nc.vector.tensor_tensor(aff[:, 5:6], gn[:, 1:2], aff[:, 5:6], ALU.subtract))
            nc.vector.tensor_scalar(aff[:, 6:8], aff[:, 4:6], SX, None, ALU.mult).then_inc(gaff_done, 1)
            dve.wait_ge(xd_done, 1)
            inner = (slice(None), slice(PAD, PAD + HH), slice(PAD, PAD + WW))
            dve.wait_ge(xh_done, 1)
            nc.vector.scalar_tensor_tensor(XL[inner], XD[inner], SX, XH[inner], ALU.mult,
                                           ALU.subtract).then_inc(xl_done, 1)

            for w in range(2):
                for half in range(2):
                    src, hi, lo = weight_split(w, half)
                    dve.wait_ge(whi_done, 2 * w + half + 1)
                    nc.vector.scalar_tensor_tensor(lo, src, SW, hi, ALU.mult, ALU.subtract).then_inc(wlo_done, 1)

            def softmax(d):
                tl = PS[:, 4 + d % 2, 0:PT * B * KK].rearrange("p (g k) -> p g k", k=KK)
                fe = FE[:, d % 2, :].rearrange("p (g k) -> p g k", k=KK)
                hi, lo = FHL[:, d, :, 0].rearrange("p (g k) -> p g k", k=KK), FHL[:, d, :, 1].rearrange("p (g k) -> p g k", k=KK)
                top = mx[:, d, :]
                dve.wait_ge(tlog_done, d + 1)
                chain(nc.vector.tensor_reduce(top, tl, AX_X, ALU.max))
                nc.vector.tensor_tensor(fe, tl, top.unsqueeze(2).to_broadcast([P, PT * B, KK]),
                                        ALU.subtract).then_inc(fsub_done, 1)
                dve.wait_ge(fexp_done, d + 1)
                chain(nc.vector.tensor_reduce(top, fe, AX_X, ALU.add))
                chain(nc.vector.reciprocal(top, top))
                chain(nc.vector.scalar_tensor_tensor(fe, fe, SF, top.unsqueeze(2).to_broadcast([P, PT * B, KK]),
                                                     ALU.mult, ALU.mult))
                chain(nc.vector.tensor_copy(hi, fe))
                nc.vector.tensor_tensor(lo, fe, hi, ALU.subtract).then_inc(fhl_done, 1)

            for d in range(ND):
                softmax(d)
            for n, (d, k) in enumerate(products):
                dve.wait_ge(fb_done, n + 1)
                if n >= NP_:
                    dve.wait_ge(acc_done, 1 + unit_of(n - NP_) + 1)
                nc.vector.tensor_tensor(plane(PR[:, n % NP_, :]), tap_view(XD, DILS[d], k),
                                        plane(banks2(2 * (n % 2))), ALU.mult).then_inc(prod_done, 1)

            dve.wait_ge(acc_done, 1 + len(units))
            for h in range(2):
                chain(nc.vector.bn_stats(st[:, h, :], bank(4 + h)))
            chain(nc.vector.bn_aggr(aff[:, 0:2], st[:, :, :].rearrange("p a b -> p (a b)")))
            nc.vector.tensor_scalar(aff[:, 1:2], aff[:, 1:2], GN_EPS, None, ALU.add).then_inc(gn2v_done, 1)
            dve.wait_ge(gn2s_done, 1)
            chain(nc.vector.reciprocal(aff[:, 3:4], aff[:, 2:3]))
            chain(nc.vector.tensor_tensor(aff[:, 4:5], aff[:, 3:4], gn[:, 2:3], ALU.mult))
            chain(nc.vector.tensor_tensor(aff[:, 5:6], aff[:, 4:5], aff[:, 0:1], ALU.mult))
            nc.vector.tensor_tensor(aff[:, 5:6], gn[:, 3:4], aff[:, 5:6], ALU.subtract).then_inc(gn2a_done, 1)

            def group_norm3(b):
                m = mv3[:, b, :]
                dve.wait_ge(y3_done, b + 1)
                for h in range(2):
                    chain(nc.vector.bn_stats(st3[:, b, h, :], bank(2 * (b % 2) + h)))
                chain(nc.vector.bn_aggr(m[:, 0:2], st3[:, b, :, :].rearrange("p a b -> p (a b)")))
                nc.vector.scalar_tensor_tensor(m[:, 1:2], m[:, 0:1], m[:, 0:1], m[:, 1:2], ALU.mult,
                                               ALU.add).then_inc(gs_done, 1)
                dve.wait_ge(gm_done, b + 1)
                chain(nc.vector.tensor_copy(m[:, 2:4], bank(4, 2)))
                chain(nc.vector.tensor_tensor(m[:, 4:5], m[:, 2:3], m[:, 2:3], ALU.mult))
                nc.vector.scalar_tensor_tensor(m[:, 4:5], m[:, 3:4], GN_EPS, m[:, 4:5], ALU.add,
                                               ALU.subtract).then_inc(gn3v_done, 1)
                dve.wait_ge(gn3s_done, b + 1)
                chain(nc.vector.reciprocal(m[:, 6:7], m[:, 5:6]))
                chain(nc.vector.tensor_tensor(m[:, 7:8], m[:, 6:7], gn[:, 4:5], ALU.mult))
                chain(nc.vector.tensor_tensor(m[:, 8:9], m[:, 7:8], m[:, 2:3], ALU.mult))
                nc.vector.tensor_tensor(m[:, 8:9], gn[:, 5:6], m[:, 8:9], ALU.subtract).then_inc(gn3a_done, 1)

            def token_stats(b):
                s = slice(b * PT, (b + 1) * PT)
                for i in range(PT):
                    if i % 2 == 0:
                        dve.wait_ge(tokc_done, (b * PT + i) // 2 + 1)
                    last = nc.vector.bn_stats(st4[:, b * PT + i, :], XTL[:, b * PT + i, 0:C])
                chain(last)
                me, ve, mo, vo = (st4[:, s, k] for k in (1, 2, 4, 5))
                chain(nc.vector.tensor_tensor(ts[:, 0, s], me, mo, ALU.subtract))
                chain(nc.vector.tensor_tensor(ts[:, 0, s], ts[:, 0, s], ts[:, 0, s], ALU.mult))
                chain(nc.vector.tensor_tensor(ts[:, 1, s], ve, vo, ALU.add))
                chain(nc.vector.scalar_tensor_tensor(ts[:, 1, s], ts[:, 0, s], C / 4.0, ts[:, 1, s], ALU.mult, ALU.add))
                nc.vector.tensor_scalar(ts[:, 1, s], ts[:, 1, s], 1.0 / C, LN_T_EPS, ALU.mult,
                                        ALU.add).then_inc(tvar_done, 1)
                chain(nc.vector.tensor_tensor(ts[:, 0, s], me, mo, ALU.add))
                dve.wait_ge(tstd_done, b + 1)
                chain(nc.vector.reciprocal(gw[:, 0, s], ts[:, 2, s]))
                chain(nc.vector.tensor_scalar(rN[:, s], gw[:, 0, s], SN, None, ALU.mult))
                nc.vector.scalar_tensor_tensor(nb[:, s], ts[:, 0, s], -0.5, rN[:, s], ALU.mult,
                                               ALU.mult).then_inc(taff_done, 1)

            def token_low(b):
                dve.wait_ge(hi_done, b + 1)
                nc.vector.tensor_tensor(XHL[:, b % 2, :, C:2 * C], XN[:, b % 2, :, :], XHL[:, b % 2, :, 0:C],
                                        ALU.subtract).then_inc(lo_done, 1)

            for b in range(B + 1):
                if b < B:
                    group_norm3(b)
                if b >= 1:
                    token_stats(b - 1)
                if b >= 2:
                    token_low(b - 2)
            def te(v):
                return v.rearrange("p (t e) -> p t e", e=E)

            def wide(v):
                return v.unsqueeze(2).to_broadcast([P, TT, E])

            L, eq, code, oh1, oh2 = (te(g8[:, k, :]) for k in range(5))
            i8 = prm_("iota8").unsqueeze(1).to_broadcast([P, TT, E])
            chain(nc.vector.tensor_tensor(L, XTL[:, :, C:C + E], wide(gw[:, 0, :]), ALU.mult))

            def largest(top, first, onehot):
                chain(nc.vector.tensor_reduce(top, L, AX_X, ALU.max))
                chain(nc.vector.tensor_tensor(eq, L, wide(top), ALU.is_equal))
                chain(nc.vector.scalar_tensor_tensor(code, eq, -float(E), i8, ALU.mult, ALU.add))
                chain(nc.vector.tensor_reduce(first, code, AX_X, ALU.min))
                chain(nc.vector.tensor_tensor(onehot, code, wide(first), ALU.is_equal))

            largest(gw[:, 1, :], gw[:, 6, :], oh1)
            token_low(B - 1)
            chain(nc.vector.scalar_tensor_tensor(L, oh1, -1e30, L, ALU.mult, ALU.add))
            largest(gw[:, 5, :], gw[:, 6, :], oh2)
            et = "p (e t) -> p t e"
            nc.vector.tensor_tensor(mask16[:, :].rearrange(et, e=E), oh1, oh2, ALU.add).then_inc(mask_done, 1)
            nc.vector.tensor_tensor(gw[:, 2, :], gw[:, 5, :], gw[:, 1, :], ALU.subtract).then_inc(gsub_done, 1)
            tot, inc, sl = g8[:, 5, :], g8[:, 6, :], g8[:, 7, :]
            dve.wait_ge(rank_done, 1)
            chain(nc.vector.tensor_copy(tot, bank(1, E * TT)))
            chain(nc.vector.tensor_tensor_scan(inc, tot, tot, 0.0, ALU.add, ALU.max))
            ends = inc.rearrange("p (e t) -> p e t", e=E)[:, :, TT - 1]
            begin, cnt, ntl, tend, off = (e8[:, k, :] for k in range(5))
            chain(nc.vector.memset(begin, 0.0))
            chain(nc.vector.tensor_copy(begin[:, 1:E], ends[:, 0:E - 1]))
            chain(nc.vector.tensor_tensor(cnt, ends, begin, ALU.subtract))
            chain(nc.vector.tensor_scalar(e8i[:, 0, :], cnt, float(P - 1), None, ALU.add))
            chain(nc.vector.tensor_scalar(e8i[:, 1, :], e8i[:, 0, :], 7, None, ALU.arith_shift_right))
            chain(nc.vector.tensor_copy(ntl, e8i[:, 1, :]))
            chain(nc.vector.tensor_tensor_scan(tend, ntl, ntl, 0.0, ALU.add, ALU.max))
            chain(nc.vector.tensor_tensor(off, tend, ntl, ALU.subtract))
            chain(nc.vector.scalar_tensor_tensor(off, off, float(P), begin, ALU.mult, ALU.subtract))
            chain(nc.vector.tensor_tensor(inc, inc, tot, ALU.subtract))
            by_e = lambda v: v.rearrange("p (e t) -> p e t", e=E)
            chain(nc.vector.tensor_tensor(by_e(inc), by_e(inc), off.unsqueeze(2).to_broadcast([P, E, TT]), ALU.add))
            chain(nc.vector.tensor_tensor(sl, inc, bank(0, E * TT), ALU.add))
            for c, oh in enumerate((oh1, oh2)):
                chain(nc.vector.tensor_tensor(code, oh, sl.rearrange(et, e=E), ALU.mult))
                chain(nc.vector.tensor_reduce(qr[:, 0, c * TT:(c + 1) * TT], code, AX_X, ALU.add))
            chain(nc.vector.tensor_copy(si[:, 0, :], qr[:, 0, :]))
            chain(nc.vector.tensor_scalar(si[:, 1, :], si[:, 0, :], 7, None, ALU.arith_shift_right))
            chain(nc.vector.tensor_scalar(si[:, 2, :], si[:, 0, :], P - 1, None, ALU.bitwise_and))
            nc.vector.tensor_copy(qr[:, 0, :], si[:, 1, :]).then_inc(qr_done, 1)
            chain(nc.vector.tensor_copy(qr[:, 1, :], si[:, 2, :]))
            dve.wait_ge(qr_done, 1)
            for n in range(2 * TT):
                nc.vector.tensor_scalar(OHR[:, n, :], k16_("iota"), qr[:, 1, n:n + 1], None, ALU.is_equal)
                nc.vector.tensor_scalar(OHQ[:, n, 0, :], k16_("iotaq"), qr[:, 0, n:n + 1], prm_("row1"), ALU.is_equal,
                                        ALU.mult).then_inc(ohr_done, 1)
            gq = ge[:, :].rearrange("p (q e) -> p q e", e=E)
            chain(nc.vector.tensor_tensor(gq, prm_("iotaq").unsqueeze(2).to_broadcast([P, NQ, E]),
                                          tend.unsqueeze(1).to_broadcast([P, NQ, E]), ALU.is_ge))
            chain(nc.vector.tensor_reduce(eid[:, :], gq, AX_X, ALU.add))
            nc.vector.tensor_scalar(eidi[:, :], eid[:, :], float(E - 1), None, ALU.min).then_inc(eid_done, 1)
            dve.wait_ge(gexp_done, 1)
            chain(nc.vector.tensor_scalar(gw[:, 7, :], gw[:, 3, :], 1.0, None, ALU.add))
            chain(nc.vector.reciprocal(gw[:, 4, :], gw[:, 7, :]))
            nc.vector.tensor_tensor(gw[:, 8, :], gw[:, 4, :], gw[:, 3, :], ALU.mult).then_inc(gates_done, 1)
            dve.wait_ge(dest_done, 1)
            chain(nc.vector.tensor_copy(dst[:, 0:2, :].rearrange("p a q -> p (a q)"), bank(4, 2 * NQ)))
            chain(nc.vector.scalar_tensor_tensor(dst[:, 2, :], dst[:, 1, :], float(P), dst[:, 0, :], ALU.mult, ALU.add))
            chain(nc.vector.tensor_scalar(dst[:, 2, :], dst[:, 2, :], -1.0, None, ALU.add))
            chain(nc.vector.tensor_scalar(dsti[:, 0, :], dst[:, 2, :], 0.0, None, ALU.max))
            chain(nc.vector.tensor_scalar(dsti[:, 1, :], dsti[:, 0, :], T - 1, None, ALU.bitwise_and))
            chain(nc.vector.tensor_scalar(dst[:, 0, :], dst[:, 2, :], 0.0, 4.0 * T, ALU.is_lt, ALU.mult))
            chain(nc.vector.tensor_tensor(dsti[:, 2, :], dst[:, 0, :], dst[:, 2, :], ALU.add))
            for q in range(3):
                nc.vector.tensor_copy(gidx[:, q:q + 1], dsti[:, 1, q:q + 1]).then_inc(gidx_ready, 1)

            def split(q, slot, lap):
                dve.wait_ge(gelu_done, q + 1)
                at_least(dve, y_done, q - 1)
                nc.vector.tensor_scalar(HS[:, slot % 2, 0, :], GF[:, slot % 2, :], SH, None, ALU.mult).then_inc(hs_done, 1)
                dve.wait_ge(hs_done, q + 1)
                nc.vector.scalar_tensor_tensor(HS[:, slot % 2, 1, :], GF[:, slot % 2, :], SH, HS[:, slot % 2, 0, :], ALU.mult,
                                               ALU.subtract).then_inc(split_done, 1)

            def finish(q, slot, lap):
                e = dve.value_load(eidi[0:1, bass.ds(q, 1)], min_val=0, max_val=E - 1)
                dve.wait_ge(y_done, q + 1)
                at_least(dve, ys_done, q - 1)
                nc.vector.scalar_tensor_tensor(YH[:, slot % 2, :], PS[:, 4 + slot % 2, C:2 * C], 1.0 / (SH * SW),
                                               B2[:, bass.ds(e * C, C)], ALU.mult, ALU.add).then_inc(yh_done, 1)
                at_least(dve, y_out[slot], 16 * lap)
                nc.vector.tensor_copy(sidx[:, slot:slot + 1], dsti[:, 2, bass.ds(q, 1)]).then_inc(yh_done, 1)
                dve.wait_ge(yh_done, 2 * (q + 1))
                nc.vector.scalar_tensor_tensor(YS[:, slot, :], PS[:, 4 + slot % 2, 0:C], 1.0 / (SH * SW), YH[:, slot % 2, :], ALU.mult,
                                               ALU.add).then_inc(ys_done, 1)

            def next_index(q, slot, lap):
                at_least(dve, g_in[slot], 16 * lap)
                nc.vector.tensor_copy(gidx[:, slot:slot + 1], dsti[:, 1, bass.ds(q, 1)]).then_inc(gidx_ready, 1)

            def step(i, j):
                if exists(tile(i, j, 3)[0]):
                    next_index(*tile(i, j, 3))
                if exists(tile(i, j)[0]):
                    split(*tile(i, j))
                if exists(tile(i, j, -1)[0]):
                    finish(*tile(i, j, -1))

            dve.wait_ge(b2_ready, 1)
            dve.wait_ge(eid_done, 1)
            run_steps(dve, step)
            for b in range(B + 1):
                if b < B:
                    for i in range(PT):
                        t = b * PT + i
                        dve.wait_ge(first_done, t + 1)
                        nc.vector.scalar_tensor_tensor(CMB[:, b % 2, i, :], YIN[:, 1, t, :], gw[:, 8, t:t + 1],
                                                       CMB[:, b % 2, i, :], ALU.mult, ALU.add).then_inc(comb_done, 1)
                if b >= 1:
                    c = b - 1
                    if c >= 2:
                        dve.wait_ge(out_done[c - 2], 16)
                    for h in range(2):
                        dve.wait_ge(ot_done, 2 * c + h + 1)
                        last = nc.vector.tensor_tensor(OUT[:, c % 2, h * HALF:(h + 1) * HALF], bank(2 * (c % 2) + h),
                                                       X[:, c * HW + h * HALF:c * HW + (h + 1) * HALF], ALU.add)
                    last.then_inc(fin_done, 1)

        @block.tensor
        def _(pe):
            pe.wait_ge(small_in, 16)
            nc.tensor.matmul(bank(7, CI + E), prm_("avg"), prm[:, COLS["w1"][0]:COLS["gate"][1]],
                             start=True, stop=True).then_inc(wmean_done, 1)

            def per_image(first_bank, lhs, rhs, done, wait=None):
                for h in range(2):
                    for b in range(B):
                        if wait:
                            wait(b)
                        last = nc.tensor.matmul(PS[b * CI:(b + 1) * CI, first_bank + h, :], lhs,
                                                rhs[:, b * HW + h * HALF:b * HW + (h + 1) * HALF], start=True, stop=True)
                    last.then_inc(done, 1)

            per_image(0, prm_("avg")[:, 0:CI], X, mean_done, lambda b: pe.wait_ge(x_in[b], 16))
            pe.wait_ge(wc_ready, 1)
            per_image(2, WC1[:, :], X, u_done)
            per_image(4, prm_("avg")[:, 0:CI], XSQ, msq_done, lambda b: pe.wait_ge(xsq_done, b + 1))

            def logits(d):
                if d >= 2:
                    pe.wait_ge(log_done, 2 * (d - 1))
                pe.wait_ge(xh_done, 1)
                for m, t in enumerate((XH, XL)):
                    if m:
                        pe.wait_ge(xl_done, 1)
                    for tap in range(KK):
                        for h in range(2):
                            last = nc.tensor.matmul(PS[0:8 * KK, 2 * (d % 2) + h, :], WCB[:, tap, d, :],
                                                    tap_view(t, DILS[d], tap, h * RH, RH),
                                                    start=(m == 0 and tap == 0), stop=(m == 1 and tap == KK - 1))
                last.then_inc(logit_done, 1)

            def turn_logits(d):
                pe.wait_ge(log_done, 2 * (d + 1))
                if d >= 2:
                    pe.wait_ge(fsub_done, d - 1)
                for i in range(PT):
                    last = nc.tensor.matmul(PS[:, 4 + d % 2, i * B * KK:(i + 1) * B * KK], LOG[0:8 * KK, d, i * P:(i + 1) * P],
                                            prm_("fold")[0:8 * KK, :], start=True, stop=True)
                last.then_inc(tlog_done, 1)

            def turn_filters(d):
                pe.wait_ge(fhl_done, d + 1)
                if d >= 2:
                    pe.wait_ge(ftc_done, d - 1)
                w = 2 * B * KK
                for i in range(PT):
                    last = nc.tensor.transpose(PS[0:w, 6 + d % 2, i * (P // 2):(i + 1) * (P // 2)].bitcast(F16),
                                               FHL[:, d, :, :].rearrange("p a b -> p (a b)")[:, i * w:(i + 1) * w],
                                               k16_("ident"))
                last.then_inc(ft_done, 1)

            pe.wait_ge(wcb_ready, 2 * B)
            logits(0)
            logits(1)
            pe.wait_ge(c16_in, 16)
            turn_logits(0)
            logits(2)
            turn_filters(0)
            turn_logits(1)
            logits(3)
            turn_filters(1)
            turn_logits(2)
            turn_logits(3)

            def spread(n):
                d, k = products[n]
                if n == 0:
                    pe.wait_ge(log_done, 8)
                if n >= 2:
                    pe.wait_ge(prod_done, n - 1)
                if k == 0:
                    pe.wait_ge(ftc_done, d + 1)
                for h in range(2):
                    last = nc.tensor.matmul(bank(2 * (n % 2) + h), k16_("sel")[0:8 * KK, k * P:(k + 1) * P],
                                            FT[0:8 * KK, d, h * HALF:(h + 1) * HALF], start=True, stop=True)
                last.then_inc(fb_done, 1)

            def accumulate(u):
                d, first, last_n = units[u]
                if last_n > first:
                    pe.wait_ge(pair_done, pairs_before(last_n))
                else:
                    pe.wait_ge(prod_done, last_n + 1)
                for h in range(2):
                    last = nc.tensor.matmul(bank(4 + h), W2B[:, 1 + d, :], PR[:, first % NP_, h * HALF:(h + 1) * HALF],
                                            start=False, stop=(u == len(units) - 1))
                last.then_inc(acc_done, 1)

            u = 0
            for n in range(len(products) + LAG):
                if n == 1:
                    turn_filters(2)
                if n == 4:
                    turn_filters(3)
                if n < len(products):
                    spread(n)
                if n == 2:
                    pe.wait_ge(w2b_ready, 2 * B)
                    pe.wait_ge(xd_done, 1)
                    pe.wait_ge(fsub_done, ND)
                    for h in range(2):
                        last = nc.tensor.matmul(bank(4 + h), W2B[:, 0, :], tap_view(XD, 1, KK // 2, h * RH, RH),
                                                start=True, stop=False)
                    last.then_inc(acc_done, 1)
                while u < len(units) and units[u][2] <= n - LAG:
                    accumulate(u)
                    u += 1

            def third_conv(b):
                if b == 0:
                    pe.wait_ge(w3z_ready, B)
                    pe.wait_ge(y2_done, 1)
                    pe.wait_ge(prod_done, len(products))
                if b >= 2:
                    pe.wait_ge(r3_done, b - 1)
                for h in range(2):
                    last = nc.tensor.matmul(bank(2 * (b % 2) + h), W3Z[:, b, :], Y2[:, h * HALF:(h + 1) * HALF],
                                            start=True, stop=True)
                last.then_inc(y3_done, 1)

            def group_means(b):
                pe.wait_ge(gs_done, b + 1)
                nc.tensor.matmul(bank(4, 2), prm_("group"), mv3[:, b, 0:2], start=True, stop=True).then_inc(gm_done, 1)

            def tokens(b):
                pe.wait_ge(x1_done, b + 1)
                for g in range(b * PT // 2, (b + 1) * PT // 2):
                    if g >= 3:
                        pe.wait_ge(tokc_done, g - 2)
                    for i in range(2):
                        t = 2 * g + i
                        last = nc.tensor.matmul(PS[:, 5 + g % 3, i * (C + E):(i + 1) * (C + E)], X[:, t * P:(t + 1) * P],
                                                RG[:, :], start=True, stop=True)
                    last.then_inc(tok_done, 1)

            third_conv(0)
            group_means(0)
            third_conv(1)
            group_means(1)
            for b in range(B):
                if b + 2 < B:
                    third_conv(b + 2)
                tokens(b)
                if b + 2 < B:
                    group_means(b + 2)
            pe.wait_ge(mask_done, 1)
            nc.tensor.matmul(bank(0, E * TT), k16_("before"), mask16[:, :], start=True, stop=True)
            nc.tensor.matmul(bank(1, E * TT), k16_("ones"), mask16[:, :], start=True, stop=True).then_inc(rank_done, 1)
            for n in range(2 * TT):
                pe.wait_ge(ohr_done, n + 1)
                pe.wait_ge(ohq_done, n + 1)
                last = nc.tensor.matmul(bank(4, 2 * NQ), OHR[:, n, :], OHQ[:, n, :, :].rearrange("p v q -> p (v q)"),
                                        start=(n == 0), stop=(n == 2 * TT - 1))
            last.then_inc(dest_done, 1)
            pe.wait_ge(eid_done, 1)
            pe.wait_ge(wlo_done, 4)

            def turn(q, slot, lap):
                pe.wait_ge(g_in[slot], 16 * (lap + 1))
                at_least(pe, xtc_done, q - 1)
                for v in range(2):
                    last = nc.tensor.transpose(PS[:, slot % 2, v * (C // 2):(v + 1) * (C // 2)].bitcast(F16),
                                               GX[:, slot, v * C:(v + 1) * C], k16_("ident"))
                last.then_inc(xt_done, 1)

            def hidden(q, slot, lap):
                e = pe.value_load(eidi[0:1, bass.ds(q, 1)], min_val=0, max_val=E - 1)
                pe.wait_ge(xtc_done, q + 1)
                at_least(pe, gelu_done, q - 1)
                hi, lo = XT[:, slot % 2, 0:C], XT[:, slot % 2, C:2 * C]
                w = W1S[:, :, :, :].rearrange("p e v n -> p (e v n)")
                for c in range(HC):
                    o = PS[:, 2 + slot % 2, c * P:(c + 1) * P]
                    whi, wlo = (w[:, bass.ds(e * (2 * HID) + v * HID + c * P, P)] for v in range(2))
                    nc.tensor.matmul(o, whi, hi, start=True, stop=False)
                    nc.tensor.matmul(o, whi, lo, start=False, stop=False)
                    last = nc.tensor.matmul(o, wlo, hi, start=False, stop=True)
                last.then_inc(h_done, 1)

            def output(q, slot, lap):
                e = pe.value_load(eidi[0:1, bass.ds(q, 1)], min_val=0, max_val=E - 1)
                pe.wait_ge(split_done, q + 1)
                at_least(pe, ys_done, q - 1)
                w = W2S[:, :, :, :].rearrange("p e v n -> p (e v n)")
                for c in range(HC):
                    at = e * (2 * HID) + c * 2 * C

                    def low():
                        nc.tensor.matmul(PS[:, 4 + slot % 2, 0:C], HS[:, slot % 2, 1, c * P:(c + 1) * P],
                                         w[:, bass.ds(at, C)], start=False, stop=False)

                    if c:
                        low()
                    last = nc.tensor.matmul(PS[:, 4 + slot % 2, 0:2 * C], HS[:, slot % 2, 0, c * P:(c + 1) * P],
                                            w[:, bass.ds(at, 2 * C)], start=(c == 0), stop=(c == HC - 1))
                    if not c:
                        low()
                last.then_inc(y_done, 1)

            turn(*tile(0, 0))

            def step(i, j):
                if exists(tile(i, j, 1)[0]):
                    turn(*tile(i, j, 1))
                if exists(tile(i, j)[0]):
                    hidden(*tile(i, j))
                if exists(tile(i, j, -1)[0]):
                    output(*tile(i, j, -1))

            run_steps(pe, step)
            for b in range(B):
                if b >= 2:
                    pe.wait_ge(fin_done, b - 1)
                for h in range(2):
                    pe.wait_ge(comb_done, b * PT + (h + 1) * PT // 2)
                    for i in range(PT // 2):
                        last = nc.tensor.transpose(PS[:, 2 * (b % 2) + h, i * P:(i + 1) * P],
                                                   CMB[:, b % 2, h * PT // 2 + i, :], prm_("ident"))
                    last.then_inc(ot_done, 1)


def kernel(**inputs):
    import concourse.bacc as _bacc
    from concourse.bass_utils import run_bass_kernel_spmd as _run

    a = {k.replace("L0_", ""): np.asarray(v) for k, v in inputs.items()}
    rep = lambda v: np.tile(v, (B, 1))
    col = lambda v, n: np.tile(v.reshape(-1, 1), (n, 1))
    wcat = np.stack([a[f"conv_w_cat{s}"].reshape(KK, CI, KK).transpose(1, 2, 0) for s in "abcd"], 2)
    c32, c16 = shape_constants()
    small = np.concatenate([
        col(a["conv_gn1_g"], B), col(a["conv_gn1_b"], B), col(a["conv_gn2_g"], B), col(a["conv_gn2_b"], B),
        col(a["conv_gn3_g"], 1), col(a["conv_gn3_b"], 1),
        a["ffn_b1"].reshape(E * HC, P).T,
        a["conv_w_scale1"].reshape(CI, C).T, a["ffn_gate_w"].T,
        rep(wcat.reshape(CI, -1)),
        rep(a["conv_w_scale2"].reshape(CI, 5, CI).transpose(2, 1, 0).reshape(CI, -1)),
        rep(a["conv_w_scale3"].reshape(C, CI).T),
        c32], 1)
    arrays = {
        "x": a["x"].reshape(B, C, HW), "small": small, "c16": c16,
        "w1t": a["ffn_w1"].transpose(2, 0, 1).reshape(P, E * HID),
        "w2t": a["ffn_w2"].reshape(E, C, HC, P).transpose(3, 0, 2, 1).reshape(P, E * HID),
        "b2": a["ffn_b2"].reshape(1, E * C),
    }
    arrays = {k: np.ascontiguousarray(v) for k, v in arrays.items()}
    nc = _bacc.Bacc("TRN2", target_bir_lowering=False, num_devices=1)
    aps = {k: nc.dram_tensor(k, v.shape, mybir.dt.from_np(v.dtype), kind="ExternalInput").ap() for k, v in arrays.items()}
    out = nc.dram_tensor("out", [B, C, HW], F32, kind="ExternalOutput").ap()
    build(nc, out=out, **aps)
    r = _run(nc, [arrays], core_ids=[0])
    return r.results[0]["out"].reshape(B, C, HH, WW)
```

```python
from contextlib import ExitStack

import concourse.bass as bass
import numpy as np
from concourse import mybir
from concourse.alu_op_type import AluOpType as ALU

ACT = mybir.ActivationFunctionType
F32 = mybir.dt.float32
F16 = mybir.dt.float16
I32 = mybir.dt.int32
U32 = mybir.dt.uint32
AX_X = mybir.AxisListType.X

P = 128
B, C, HH, WW = 4, 128, 32, 32
HW = HH * WW
T = B * HW
CI = 32
KK = 9
DILS = (1, 4, 8, 12)
ND = len(DILS)
PAD = max(DILS)
WP = HH + 2 * PAD
HALF = HW // 2
RH = HH // 2
PT = HW // P
TT = T // P
E, HID = 8, 512
HC = HID // P
NQ = (2 * T + E * (P - 1)) // P
LN_C_EPS, GN_EPS, LN_T_EPS = 1e-6, 1e-5, 1e-5

SX = 2.0 ** 7
SW = 2.0 ** 8
SF = 2.0 ** 12
SN = 2.0 ** 11
SH = 2.0 ** 6

COLS = {}


def _cols():
    at = 0
    for name, n in (("gn", 6), ("b1", E * HC), ("w1", CI), ("gate", E), ("wcat", KK * ND * KK), ("w2", 5 * CI),
                    ("w3", C), ("ident", P), ("avg", P), ("group", P), ("fold", 4 * KK), ("iota8", E),
                    ("iotaq", NQ), ("row1", 1)):
        COLS[name] = (at, at + n)
        at += n
    return at


NS = _cols()
C16 = {"ident": (0, P), "before": (P, 2 * P), "ones": (2 * P, 3 * P), "iota": (3 * P, 4 * P),
       "iotaq": (4 * P, 4 * P + NQ), "sel": (4 * P + NQ, 4 * P + NQ + KK * P)}
NC16 = C16["sel"][1]


def shape_constants():
    c32 = np.zeros((P, NS - COLS["ident"][0]), np.float32)
    base = COLS["ident"][0]

    def put(name, value, rows=P):
        a, b = COLS[name]
        c32[:rows, a - base:b - base] = value

    put("ident", np.eye(P))
    put("avg", 1.0 / C)
    put("group", np.kron(np.eye(C // 4), np.full((4, 4), 0.25)))
    put("fold", np.concatenate([np.eye(4 * KK), np.eye(4 * KK)]), 8 * KK)
    put("iota8", np.arange(E))
    put("iotaq", np.arange(NQ))
    put("row1", np.arange(1, P + 1)[:, None])
    c16 = np.zeros((P, NC16), np.float16)
    c16[:, 0:P] = np.eye(P)
    c16[:, P:2 * P] = np.triu(np.ones((P, P)), 1)
    c16[:, 2 * P:3 * P] = 1.0
    c16[:, 3 * P:4 * P] = np.arange(P)
    c16[:, 4 * P:4 * P + NQ] = np.arange(NQ)
    sel = np.zeros((B, KK, 2, KK, B, CI), np.float16)
    for b in range(B):
        for k in range(KK):
            sel[b, k, :, k, b, :] = 1.0
    c16[:B * KK * 2, 4 * P + NQ:] = sel.reshape(B * KK * 2, KK * P)
    return c32, c16


def build(nc, x, small, c16, w1t, w2t, b2, out):
    ctx = ExitStack()
    with ctx:
        def sb(name, shape, dt=F32):
            return ctx.enter_context(nc.sbuf_tensor(name, shape, dt))

        def sem(name):
            return ctx.enter_context(nc.semaphore(name))

        X = sb("X", [P, T])
        prm = sb("prm", [P, NS])
        k16 = sb("k16", [P, NC16], F16)
        WST = sb("WST", [P, 2, E * HID])
        W1S = sb("W1S", [P, E, 2, HID], F16)
        W2S = sb("W2S", [P, E, 2, HID], F16)
        B2 = sb("B2", [P, E * C])
        RG = sb("RG", [P, P + E])
        WC1 = sb("WC1", [P, CI])
        WCS = sb("WCS", [P, 2, KK * ND * KK], F16)
        WCB = sb("WCB", [P, KK, ND, 8 * KK], F16)
        W2B = sb("W2B", [P, 5, P])
        W3Z = sb("W3Z", [P, B, P])
        MV = sb("MV", [P, 4, HW])
        MSQ, VAR, LOG = MV[:, 0, :], MV[:, 1, :], MV[:, 2:4, :]
        XHL = MV[:, :, :].rearrange("p a n -> p (a n)").bitcast(F16).rearrange(
            "p (b i n) -> p b i n", b=B, i=PT)
        Z = sb("Z", [P, HW])
        RX = sb("RX", [P, 2 * WP * WP])
        XD = RX[:, 0:WP * WP].rearrange("p (h w) -> p h w", w=WP)
        XH = RX[:, WP * WP:3 * WP * WP // 2].bitcast(F16).rearrange("p (h w) -> p h w", w=WP)
        XL = RX[:, 3 * WP * WP // 2:2 * WP * WP].bitcast(F16).rearrange("p (h w) -> p h w", w=WP)
        XTL = RX[:, 0:TT * (C + E)].rearrange("p (t n) -> p t n", t=TT)
        st = sb("st", [P, 2, 6])
        aff = sb("aff", [P, 16])
        FE = sb("FE", [P, 2, PT * B * KK])
        mx = sb("mx", [P, ND, PT * B])
        FHL = sb("FHL", [P, ND, PT * B * KK, 2], F16)
        FT = sb("FT", [P, ND, HW], F16)
        PR = sb("PR", [P, 8, HW])
        SUM1, SUM2, RING, OWN = PR[:, 0:2, :], PR[:, 2:4, :], PR[:, 4:7, :], PR[:, 7, :]
        R3 = PR[:, 0:4, :]
        XN = PR[:, 4:8, :].rearrange("p s (i n) -> p s i n", n=C)
        XSQ = PR[:, 0:T // HW, :].rearrange("p a n -> p (a n)")
        Y2 = Z
        Y3_BANK = (0, 2, 6, 0)
        TOKEN_BANK = (5, 2, 3)
        OHR = WST[:, 0, :].bitcast(F16).rearrange("p (n r) -> p n r", r=P)
        OHQ = PR[:, :, :].rearrange("p a n -> p (a n)")[:, 0:2 * TT * NQ].bitcast(F16).rearrange(
            "p (n v q) -> p n v q", v=2, q=NQ)
        OHN = 16
        YIN = WST[:, :, :].rearrange("p j (t c) -> p j t c", c=C)
        CMB = PR[:, 0:2, :].rearrange("p s (i n) -> p s i n", n=C)
        OUT = PR[:, 2:4, :]
        st3 = sb("st3", [P, B, 2, 6])
        mv3 = sb("mv3", [P, 10, B])
        st4 = sb("st4", [P, TT, 6])
        ts = sb("ts", [P, 5, TT])
        rN, nb = ts[:, 3, :], ts[:, 4, :]
        gw = sb("gw", [P, 12, TT])
        g8 = FT[:, :, :].rearrange("p d n -> p (d n)").bitcast(F32).rearrange("p (k n) -> p k n", k=8)
        mask16 = sb("mask16", [P, E * TT], F16)
        e8 = sb("e8", [P, 8, E])
        e8i = sb("e8i", [P, 2, E], I32)
        si = sb("si", [P, 3, 2 * TT], I32)
        qr = sb("qr", [P, 2, 2 * TT])
        q16 = sb("q16", [P, 2 * TT], F16)
        ge = FHL[:, :, :, :].rearrange("p d g v -> p (d g v)").bitcast(F32)[:, 0:NQ * E]
        eid = sb("eid", [P, NQ])
        eidi = sb("eidi", [P, NQ], I32)
        dst = sb("dst", [P, 3, NQ])
        dsti = sb("dsti", [P, 3, NQ], I32)
        NR = 8
        gidx, sidx = sb("gidx", [P, NR], I32), sb("sidx", [P, NR], I32)
        GX = PR[:, 6, :].bitcast(F16).rearrange("p (r n) -> p r n", r=NR)
        XT = sb("XT", [P, 2, 2 * C], F16)
        GF = WCB[:, :, :, :].rearrange("p t d m -> p (t d m)").bitcast(F32)[:, 0:2 * HID].rearrange("p (s n) -> p s n", s=2)
        HS = RX[:, TT * (C + E):TT * (C + E) + 2 * HID].bitcast(F16).rearrange("p (s v n) -> p s v n", s=2, v=2)
        YH = sb("YH", [P, 2, C])
        YS = PR[:, 5, :].rearrange("p (r n) -> p r n", r=NR)
        PS = ctx.enter_context(nc.psum_tensor("PS", [P, 8, 512], F32))

        xr = nc.dram_tensor("token_rows", [T, 2 * C], F16).ap()
        yr = nc.dram_tensor("expert_rows", [2 * T, C], F32).ap()

        def prm_(name):
            a, b = COLS[name]
            return prm[:, a:b]

        def k16_(name):
            a, b = C16[name]
            return k16[:, a:b]

        def bank(i, n=512):
            return PS[:, i, 0:n]

        def banks2(i):
            return PS[:, i:i + 2, :].rearrange("p a n -> p (a n)")

        def tap_view(t, d, k, r0=0, rows=HH):
            oy, ox = PAD + d * (k // 3 - 1) + r0, PAD + d * (k % 3 - 1)
            return t[:, oy:oy + rows, ox:ox + WW]

        def plane(v):
            return v.rearrange("p (h w) -> p h w", w=WW)

        small_in, c16_in, w_in, b2_in = sem("small_in"), sem("c16_in"), sem("w_in"), sem("b2_in")
        x_in = [sem(f"x_in{b}") for b in range(B)]
        wmean_done = sem("wmean_done")
        wc_ready = sem("wc_ready")
        wcb_ready, w2b_ready, w3z_ready = sem("wcb_ready"), sem("w2b_ready"), sem("w3z_ready")
        zero_done = sem("zero_done")
        xsq_done = sem("xsq_done")
        mean_done, u_done, msq_done = sem("mean_done"), sem("u_done"), sem("msq_done")
        mean2_done, var_done, std_done = sem("mean2_done"), sem("var_done"), sem("std_done")
        gvar_done, gstd_done, gaff_done = sem("gvar_done"), sem("gstd_done"), sem("gaff_done")
        xd_done, xh_done, xl_done = sem("xd_done"), sem("xh_done"), sem("xl_done")
        logit_done, log_done, tlog_done = sem("logit_done"), sem("log_done"), sem("tlog_done")
        fsub_done, fexp_done, fhl_done = sem("fsub_done"), sem("fexp_done"), sem("fhl_done")
        ft_done, ftc_done = sem("ft_done"), sem("ftc_done")
        fb_done, prod_done, acc_done = sem("fb_done"), sem("prod_done"), sem("acc_done")
        ring_used, sum2_done, own_used = sem("ring_used"), sem("sum2_done"), sem("own_used")
        gln_done, gn2l_done, gn3l_done, tln_done = sem("gln_done"), sem("gn2l_done"), sem("gn3l_done"), sem("tln_done")
        oh_done = sem("oh_done")
        ln_done = sem("ln_done")
        gn2v_done, gn2s_done, gn2a_done, y2_done = sem("gn2v_done"), sem("gn2s_done"), sem("gn2a_done"), sem("y2_done")
        y3_done, gs_done, gm_done = sem("y3_done"), sem("gs_done"), sem("gm_done")
        gn3v_done, gn3s_done, gn3a_done = sem("gn3v_done"), sem("gn3s_done"), sem("gn3a_done")
        r3_done, x1_done = sem("r3_done"), [sem(f"x1_done{b}") for b in range(B)]
        tok_done, tokc_done = sem("tok_done"), sem("tokc_done")
        tvar_done, tstd_done, taff_done = sem("tvar_done"), sem("tstd_done"), sem("taff_done")
        xn_done, hi_done, lo_done, rows_out = sem("xn_done"), sem("hi_done"), sem("lo_done"), [sem(f"rows_out{b}") for b in range(B)]
        gsub_done, gexp_done = sem("gsub_done"), sem("gexp_done")
        mask_done, rank_done = sem("mask_done"), sem("rank_done")
        qr_done, ohr_done, ohq_done, row_ready = sem("qr_done"), sem("ohr_done"), sem("ohq_done"), sem("row_ready")
        dest_done, eid_done = sem("dest_done"), sem("eid_done")
        whi_done, wlo_done, b2_ready = sem("whi_done"), sem("wlo_done"), sem("b2_ready")
        gidx_ready = sem("gidx_ready")
        g_in = [sem(f"g_in{j}") for j in range(8)]
        y_out = [sem(f"y_out{j}") for j in range(8)]
        xt_done, xtc_done, h_done, gelu_done = sem("xt_done"), sem("xtc_done"), sem("h_done"), sem("gelu_done")
        split_done, y_done, ys_done = sem("split_done"), sem("y_done"), sem("ys_done")
        y_in = [sem(f"y_in{b}") for b in range(B)]
        first_done, comb_done, ot_done, fin_done = sem("first_done"), sem("comb_done"), sem("ot_done"), sem("fin_done")
        gates_done = sem("gates_done")
        hs_done, yh_done = sem("hs_done"), sem("yh_done")
        dve_step, act_step, pool_step = sem("dve_step"), sem("act_step"), sem("pool_step")
        out_done = [sem(f"out_done{b}") for b in range(B)]
        pool_held = sem("pool_held")

        NPR = ND * KK
        DVE_TAPS, POOL_TAPS = (3, 6), (2, 4, 5, 7, 8)

        FB_BANK = (2, 3, 4)
        FIRST_TAPS = 5
        ACC_AFTER = 5
        work = [(1, tap) for tap in range(FIRST_TAPS, KK)] + [(d, tap) for d in (2, 3) for tap in range(KK)]
        BESIDE = [[] for _ in range(NPR)]
        for i, w in enumerate(work):
            BESIDE[i].append(w)
        TOP_AT = {d: 1 + (d - 1) * KK + KK - FIRST_TAPS for d in range(1, ND)}

        def pool_taps_before(n):
            return (n // KK) * len(POOL_TAPS) + sum(1 for k in POOL_TAPS if k < n % KK)

        def product_buffer(n):
            d, k = n // KK, n % KK
            if k == 0:
                return SUM1[:, d % 2, :]
            if k == 1:
                return SUM2[:, d % 2, :]
            return OWN if k in DVE_TAPS else RING[:, pool_taps_before(n) % 3, :]

        def weight_split(w, half):
            n = (HID, C)[w]
            src = WST[:, w, :].rearrange("p (g n) -> p g n", n=n)
            dest = (W1S, W2S)[w][:, :, :, :].rearrange("p e v n -> p (e v n)").rearrange("p (g v n) -> p g v n", v=2, n=n)
            g = src.shape[1] // 2
            s = slice(half * g, (half + 1) * g)
            return src[:, s, :], dest[:, s, 0, :], dest[:, s, 1, :]

        SLAG = 5
        ILAG = 6
        NSTEP = NQ + 1

        def run_steps(engine, step):
            laps = (NSTEP - 1) // NR
            for s in range(2 * NR):
                step(s // NR, s % NR)
            with engine.Fori(2, laps) as i:
                for j in range(NR):
                    step(i, j)
            for s in range(NR * laps, NSTEP):
                step(s // NR, s % NR)

        def tile(i, j, ahead=0):
            return NR * i + (j + ahead), (j + ahead) % NR, i + (j + ahead) // NR

        def exists(q):
            return not isinstance(q, int) or 0 <= q < NQ

        def at_least(engine, signal, value):
            if not isinstance(value, int) or value > 0:
                engine.wait_ge(signal, value)

        block = ctx.enter_context(nc.Block())

        @block.sync
        def _(sp):
            sp.dma_start(prm[:, :], small).then_inc(small_in, 16)
            for b in (1, 3):
                sp.dma_start(X[:, b * HW:(b + 1) * HW], x[b]).then_inc(x_in[b], 16)
            sp.dma_start(WST[:, 0, :], w1t).then_inc(w_in, 16)
            sp.dma_start(B2[0:1, :], b2).then_inc(b2_in, 16)
            for b in range(B):
                sp.wait_ge(hi_done, b + 1)
                sp.wait_ge(lo_done, b + 1)
                sp.dma_start(xr[b * HW:(b + 1) * HW, :].rearrange("(i p) n -> p i n", p=P),
                             XHL[:, b, :, :]).then_inc(rows_out[b], 16)
            for j in range(NR):
                sp.wait_ge(y_out[j], 16 * ((NQ - 1 - j) // NR + 1))
            for b in range(B):
                for c in range(2):
                    sp.dma_start(YIN[:, c, b * PT:(b + 1) * PT, :], yr[c * T + b * HW:c * T + (b + 1) * HW, :].rearrange(
                        "(i p) n -> p i n", p=P)).then_inc(y_in[b], 16)
            for b in range(B):
                sp.wait_ge(fin_done, b + 1)
                sp.dma_start(out[b], OUT[:, b % 2, :]).then_inc(out_done[b], 16)
            for b in range(B):
                sp.wait_ge(out_done[b], 16)

        @block.gpsimd
        def _(pool):
            for t in (XD, XH, XL, WCB, W2B, W3Z):
                ap = t[:, :, :] if len(t.shape) == 3 else t[:, :, :, :].rearrange("p a b c -> p a (b c)")
                nc.gpsimd.memset(ap, 0.0).then_inc(zero_done, 1)
            pool.wait_ge(b2_in, 16)
            nc.gpsimd.partition_broadcast(B2[:, :], B2[0:1, :]).then_inc(b2_ready, 1)
            for d in range(ND):
                for k in POOL_TAPS:
                    n = d * KK + k
                    pool.wait_ge(prod_done, 2 * n + 2)
                    if k > POOL_TAPS[0]:
                        pool.wait_ge(ring_used, pool_taps_before(n))
                    nc.gpsimd.tensor_tensor(SUM2[:, d % 2, :], SUM2[:, d % 2, :], product_buffer(n),
                                            ALU.add).then_inc(ring_used, 1)
                pool.wait_ge(ring_used, (d + 1) * len(POOL_TAPS))
                pool.wait_ge(own_used, 2 * (d + 1))
                nc.gpsimd.tensor_tensor(SUM2[:, d % 2, :], SUM2[:, d % 2, :], SUM1[:, d % 2, :],
                                        ALU.add).then_inc(sum2_done, 1)
            for b in (1, 3):
                s = slice(b * HW, (b + 1) * HW)
                pool.wait_ge(r3_done, b + 1)
                nc.gpsimd.tensor_tensor(X[:, s], X[:, s], R3[:, b, :], ALU.add).then_inc(x1_done[b], 1)
            for b in range(B):
                pool.wait_ge(hi_done, b + 1)
                nc.gpsimd.tensor_tensor(XHL[:, b, :, C:2 * C], XN[:, b, :, :], XHL[:, b, :, 0:C],
                                        ALU.subtract).then_inc(lo_done, 1)
            for b in range(B):
                pool.wait_ge(rows_out[b], 16)

            def gather(q, slot, lap):
                pool.wait_ge(gidx_ready, q + 1)
                at_least(pool, xt_done, q - NR + 1)
                pool.sem_inc(pool_held, 1)
                nc.gpsimd.indirect_dma_start(GX[:, slot, :], None, xr, bass.IndirectOffsetOnAxis(
                    ap=gidx[:, slot:slot + 1].bitcast(U32), axis=0)).then_inc(g_in[slot], 16)

            def scatter(q, slot, lap):
                pool.wait_ge(ys_done, q + 1)
                pool.sem_inc(pool_held, 1)
                nc.gpsimd.indirect_dma_start(yr, bass.IndirectOffsetOnAxis(ap=sidx[:, slot:slot + 1].bitcast(U32), axis=0),
                                             YS[:, slot, :], None, bounds_check=2 * T - 1,
                                             oob_is_err=False).then_inc(y_out[slot], 16)

            def step(i, j):
                if exists(tile(i, j)[0]):
                    gather(*tile(i, j))
                if exists(tile(i, j, -SLAG)[0]):
                    scatter(*tile(i, j, -SLAG))

            run_steps(pool, step)
            for q in range(NSTEP - SLAG, NQ):
                scatter(q, q % NR, q // NR)

        @block.scalar
        def _(act):
            steps = [0]

            def inverse_std(out_, var, done):
                steps[0] += 1
                nc.scalar.activation(out_, var, ACT.Ln).then_inc(ln_done, 1)
                act.wait_ge(ln_done, steps[0])
                nc.scalar.activation(out_, out_, ACT.Exp, scale=-0.5).then_inc(done, 1)

            for b in (0, 2):
                act.dma_start(X[:, b * HW:(b + 1) * HW], x[b]).then_inc(x_in[b], 16)
            act.dma_start(k16[:, :], c16).then_inc(c16_in, 16)
            act.dma_start(WST[:, 1, :], w2t).then_inc(w_in, 16)
            for b in range(B):
                act.wait_ge(x_in[b], 16)
                nc.scalar.activation(XSQ[:, b * HW:(b + 1) * HW], X[:, b * HW:(b + 1) * HW],
                                     ACT.Square).then_inc(xsq_done, 1)
            for h in range(2):
                act.wait_ge(mean_done, h + 1)
                nc.scalar.activation(MSQ[:, h * HALF:(h + 1) * HALF], bank(h), ACT.Square).then_inc(mean2_done, 1)
            for h in range(2):
                act.wait_ge(var_done, h + 1)
                inverse_std(MSQ[:, h * HALF:(h + 1) * HALF], VAR[:, h * HALF:(h + 1) * HALF], std_done)
            act.wait_ge(gvar_done, 1)
            inverse_std(aff[:, 3:4], aff[:, 1:2], gstd_done)
            act.wait_ge(gaff_done, 1)
            act.wait_ge(zero_done, 3)
            nc.scalar.activation(XH[:, PAD:PAD + HH, PAD:PAD + WW], plane(Z[:, :]), ACT.Relu,
                                 bias=aff[:, 7:8], scale=aff[:, 6:7]).then_inc(xh_done, 1)
            nc.scalar.activation(XD[:, PAD:PAD + HH, PAD:PAD + WW], plane(Z[:, :]), ACT.Relu,
                                 bias=aff[:, 5:6], scale=aff[:, 4:5]).then_inc(xd_done, 1)

            def evacuate_logits(d):
                act.wait_ge(logit_done, d + 1)
                if d >= 2:
                    act.wait_ge(tlog_done, d - 1)
                for h in range(2):
                    nc.scalar.activation(LOG[0:8 * KK, d % 2, h * HALF:(h + 1) * HALF], PS[0:8 * KK, h, :],
                                         ACT.Copy, scale=1.0 / (SX * SW)).then_inc(log_done, 1)

            def exponential(d):
                act.wait_ge(fsub_done, d + 1)
                nc.scalar.activation(FE[:, d % 2, :], FE[:, d % 2, :], ACT.Exp).then_inc(fexp_done, 1)

            def evacuate_filters(d):
                act.wait_ge(ft_done, d + 1)
                nc.scalar.activation(FT[0:8 * KK, d, :], PS[0:8 * KK, 5, :].bitcast(F16), ACT.Copy).then_inc(ftc_done, 1)

            act.wait_ge(w_in, 32)
            for w in range(2):
                for half in range(2):
                    src, hi, _ = weight_split(w, half)
                    nc.scalar.activation(hi, src, ACT.Copy, scale=SW).then_inc(whi_done, 1)
            for d in range(ND):
                evacuate_logits(d)
                exponential(d)
                evacuate_filters(d)
            act.wait_ge(gn2v_done, 1)
            inverse_std(aff[:, 3:4], aff[:, 1:2], gn2s_done)
            act.wait_ge(gn2a_done, 1)
            nc.scalar.activation(Y2[:, :], banks2(6), ACT.Relu, bias=aff[:, 5:6], scale=aff[:, 4:5]).then_inc(y2_done, 1)

            def relu3(images):
                part = slice(images[0], images[-1] + 1)
                act.wait_ge(gn3v_done, images[-1] + 1)
                inverse_std(mv3[:, 5, part], mv3[:, 4, part], gn3s_done)
                act.wait_ge(gn3a_done, images[-1] + 1)
                for b in images:
                    nc.scalar.activation(R3[:, b, :], banks2(Y3_BANK[b]), ACT.Relu,
                                         bias=mv3[:, 8, b:b + 1], scale=mv3[:, 7, b:b + 1]).then_inc(r3_done, 1)

            def evacuate_tokens(b):
                for g in range(b * PT // 2, (b + 1) * PT // 2):
                    act.wait_ge(tok_done, g + 1)
                    nc.scalar.activation(XTL[:, 2 * g:2 * g + 2, :].rearrange("p a n -> p (a n)"),
                                         PS[:, TOKEN_BANK[g % 3], 0:2 * (C + E)], ACT.Copy).then_inc(tokc_done, 1)

            def token_scale(b):
                act.wait_ge(tvar_done, b + 1)
                inverse_std(gw[:, 0, b * PT:(b + 1) * PT], ts[:, 1, b * PT:(b + 1) * PT], tstd_done)

            def token_high(b):
                act.wait_ge(xn_done, PT * (b + 1))
                nc.scalar.activation(XHL[:, b, :, 0:C], XN[:, b, :, :], ACT.Copy).then_inc(hi_done, 1)

            relu3((0, 1, 2))
            evacuate_tokens(0)
            relu3((3,))
            token_scale(0)
            for b in range(1, B):
                evacuate_tokens(b)
                token_high(b - 1)
                token_scale(b)
            token_high(B - 1)
            act.wait_ge(gsub_done, 1)
            nc.scalar.activation(gw[:, 3, :], gw[:, 2, :], ACT.Exp).then_inc(gexp_done, 1)
            for n in range(2 * TT):
                act.wait_ge(oh_done, n // OHN + 1)
                nc.scalar.activation(OHQ[:, n, 1, :], OHQ[:, n, 1, :], ACT.Copy, scale=float(n)).then_inc(ohq_done, 1)
            act.wait_ge(eid_done, 1)
            b1 = prm_("b1").rearrange("p (e c) -> p e c", c=HC)

            def turned(q, slot, lap):
                act.wait_ge(xt_done, q + 1)
                at_least(act, h_done, q - 1)
                nc.scalar.activation(XT[:, slot % 2, :], PS[:, slot % 2, 0:C].bitcast(F16), ACT.Copy).then_inc(xtc_done, 1)

            def gelu(q, slot, lap):
                e = act.value_load(eidi[0:1, bass.ds(q, 1)], min_val=0, max_val=E - 1)
                act.wait_ge(h_done, q + 1)
                at_least(act, split_done, q - 1)
                for c in range(HC):
                    last = nc.scalar.activation(GF[:, slot % 2, c * P:(c + 1) * P], PS[:, 2 + slot % 2, c * P:(c + 1) * P],
                                                ACT.Gelu, bias=b1[:, bass.ds(e, 1), c], scale=1.0 / (SN * SW))
                last.then_inc(gelu_done, 1)

            turned(*tile(0, 0))

            def step(i, j):
                if exists(tile(i, j, 1)[0]):
                    turned(*tile(i, j, 1))
                if exists(tile(i, j)[0]):
                    gelu(*tile(i, j))

            run_steps(act, step)
            for t in range(TT):
                if t % PT == 0:
                    act.wait_ge(y_in[t // PT], 32)
                    if t // PT >= 2:
                        act.wait_ge(ot_done, 2 * (t // PT - 1))
                if t == 0:
                    act.wait_ge(gates_done, 1)
                nc.scalar.activation(CMB[:, (t // PT) % 2, t % PT, :], YIN[:, 0, t, :], ACT.Copy,
                                     scale=gw[:, 4, t:t + 1]).then_inc(first_done, 1)

        @block.vector
        def _(dve):
            steps = [0]

            def chain(ins):
                steps[0] += 1
                ins.then_inc(dve_step, 1)
                dve.wait_ge(dve_step, steps[0])

            dve.wait_ge(small_in, 16)
            a, g = COLS["w1"][0], COLS["gate"][0]
            nc.vector.tensor_copy(RG[:, 0:P], prm_("ident"))
            dve.wait_ge(wmean_done, 1)
            nc.vector.tensor_tensor(WC1[:, :], prm_("w1"), bank(7, CI), ALU.subtract).then_inc(wc_ready, 1)
            nc.vector.tensor_tensor(RG[:, P:P + E], prm_("gate"), PS[:, 7, CI:CI + E], ALU.subtract).then_inc(wc_ready, 1)
            chain(nc.vector.tensor_scalar(WCS[:, 0, :], prm_("wcat"), SW, None, ALU.mult))
            chain(nc.vector.scalar_tensor_tensor(WCS[:, 1, :], prm_("wcat"), SW, WCS[:, 0, :], ALU.mult, ALU.subtract))
            dve.wait_ge(zero_done, 6)
            for b in range(B):
                rows = slice(b * CI, (b + 1) * CI)
                for s in range(2):
                    o = 4 * KK * s + KK * b
                    nc.vector.tensor_copy(WCB[rows, :, :, o:o + KK], WCS[rows, s, :].rearrange(
                        "p (t d k) -> p t d k", t=KK, d=ND)).then_inc(wcb_ready, 1)
                w2 = prm_("w2").rearrange("p (s o) -> p s o", s=5)
                nc.vector.tensor_copy(W2B[rows, 0, b * CI:(b + 1) * CI], w2[rows, 0, :]).then_inc(w2b_ready, 1)
                nc.vector.tensor_scalar(W2B[rows, 1:5, b * CI:(b + 1) * CI], w2[rows, 1:5, :], 1.0 / SF, None,
                                        ALU.mult).then_inc(w2b_ready, 1)
                nc.vector.tensor_copy(W3Z[rows, b, :], prm_("w3")[rows, :]).then_inc(w3z_ready, 1)
            for h in range(2):
                s = slice(h * HALF, (h + 1) * HALF)
                dve.wait_ge(mean2_done, h + 1)
                dve.wait_ge(msq_done, h + 1)
                nc.vector.scalar_tensor_tensor(VAR[:, s], bank(4 + h), LN_C_EPS, MSQ[:, s], ALU.add,
                                               ALU.subtract).then_inc(var_done, 1)
            for h in range(2):
                s = slice(h * HALF, (h + 1) * HALF)
                dve.wait_ge(std_done, h + 1)
                dve.wait_ge(u_done, h + 1)
                chain(nc.vector.tensor_tensor(Z[:, s], bank(2 + h), MSQ[:, s], ALU.mult))
                chain(nc.vector.bn_stats(st[:, h, :], Z[:, s]))
            gn = prm_("gn")
            chain(nc.vector.bn_aggr(aff[:, 0:2], st[:, :, :].rearrange("p a b -> p (a b)")))
            nc.vector.tensor_scalar(aff[:, 1:2], aff[:, 1:2], GN_EPS, None, ALU.add).then_inc(gvar_done, 1)
            dve.wait_ge(gstd_done, 1)
            chain(nc.vector.tensor_tensor(aff[:, 4:5], aff[:, 3:4], gn[:, 0:1], ALU.mult))
            chain(nc.vector.tensor_tensor(aff[:, 5:6], aff[:, 4:5], aff[:, 0:1], ALU.mult))
            chain(nc.vector.tensor_tensor(aff[:, 5:6], gn[:, 1:2], aff[:, 5:6], ALU.subtract))
            nc.vector.tensor_scalar(aff[:, 6:8], aff[:, 4:6], SX, None, ALU.mult).then_inc(gaff_done, 1)
            dve.wait_ge(xd_done, 1)
            inner = (slice(None), slice(PAD, PAD + HH), slice(PAD, PAD + WW))
            dve.wait_ge(xh_done, 1)
            nc.vector.scalar_tensor_tensor(XL[inner], XD[inner], SX, XH[inner], ALU.mult,
                                           ALU.subtract).then_inc(xl_done, 1)

            for w in range(2):
                for half in range(2):
                    src, hi, lo = weight_split(w, half)
                    dve.wait_ge(whi_done, 2 * w + half + 1)
                    nc.vector.scalar_tensor_tensor(lo, src, SW, hi, ALU.mult, ALU.subtract).then_inc(wlo_done, 1)

            def softmax_top(d):
                tl = PS[:, 5, 0:PT * B * KK].rearrange("p (g k) -> p g k", k=KK)
                fe = FE[:, d % 2, :].rearrange("p (g k) -> p g k", k=KK)
                dve.wait_ge(tlog_done, d + 1)
                chain(nc.vector.tensor_reduce(mx[:, d, :], tl, AX_X, ALU.max))
                nc.vector.tensor_tensor(fe, tl, mx[:, d, :].unsqueeze(2).to_broadcast([P, PT * B, KK]),
                                        ALU.subtract).then_inc(fsub_done, 1)

            def softmax_end(d):
                fe = FE[:, d % 2, :].rearrange("p (g k) -> p g k", k=KK)
                hi, lo = (FHL[:, d, :, v].rearrange("p (g k) -> p g k", k=KK) for v in range(2))
                dve.wait_ge(fexp_done, d + 1)
                chain(nc.vector.tensor_reduce(mx[:, d, :], fe, AX_X, ALU.add))
                chain(nc.vector.reciprocal(mx[:, d, :], mx[:, d, :]))
                chain(nc.vector.scalar_tensor_tensor(fe, fe, SF, mx[:, d, :].unsqueeze(2).to_broadcast([P, PT * B, KK]),
                                                     ALU.mult, ALU.mult))
                chain(nc.vector.tensor_copy(hi, fe))
                nc.vector.tensor_tensor(lo, fe, hi, ALU.subtract).then_inc(fhl_done, 1)

            softmax_top(0)
            softmax_end(0)
            for n in range(NPR):
                d, k = n // KK, n % KK
                for d2 in range(1, ND):
                    if n == TOP_AT[d2]:
                        softmax_top(d2)
                    if n == TOP_AT[d2] + 1:
                        softmax_end(d2)
                buffer = product_buffer(n)
                if k == 0 and d >= 2:
                    dve.wait_ge(sum2_done, d - 1)
                if k == 1 and d >= 2:
                    dve.wait_ge(acc_done, 1 + d - 1)
                if k in POOL_TAPS and pool_taps_before(n) >= 3:
                    dve.wait_ge(ring_used, pool_taps_before(n) - 2)
                if n > DVE_TAPS[0] and k in DVE_TAPS:
                    dve.wait_ge(own_used, 2 * d + DVE_TAPS.index(k))
                for h in range(2):
                    dve.wait_ge(fb_done, 2 * n + h + 1)
                    nc.vector.tensor_tensor(plane(buffer[:, h * HALF:(h + 1) * HALF]),
                                            tap_view(XD, DILS[d], k, h * RH, RH),
                                            plane(bank(FB_BANK[(2 * n + h) % 3])), ALU.mult).then_inc(prod_done, 1)
                if k in DVE_TAPS:
                    dve.wait_ge(prod_done, 2 * n + 2)
                    if k == DVE_TAPS[1]:
                        dve.wait_ge(own_used, 2 * d + 1)
                    nc.vector.tensor_tensor(SUM1[:, d % 2, :], SUM1[:, d % 2, :], OWN, ALU.add).then_inc(own_used, 1)

            dve.wait_ge(acc_done, 1 + ND)
            for h in range(2):
                chain(nc.vector.bn_stats(st[:, h, :], bank(6 + h)))
            chain(nc.vector.bn_aggr(aff[:, 0:2], st[:, :, :].rearrange("p a b -> p (a b)")))
            nc.vector.tensor_scalar(aff[:, 1:2], aff[:, 1:2], GN_EPS, None, ALU.add).then_inc(gn2v_done, 1)
            dve.wait_ge(gn2s_done, 1)
            chain(nc.vector.tensor_tensor(aff[:, 4:5], aff[:, 3:4], gn[:, 2:3], ALU.mult))
            chain(nc.vector.tensor_tensor(aff[:, 5:6], aff[:, 4:5], aff[:, 0:1], ALU.mult))
            nc.vector.tensor_tensor(aff[:, 5:6], gn[:, 3:4], aff[:, 5:6], ALU.subtract).then_inc(gn2a_done, 1)

            def channel_stats(b):
                dve.wait_ge(y3_done, b + 1)
                for h in range(2):
                    last = nc.vector.bn_stats(st3[:, b, h, :], bank(Y3_BANK[b] + h))
                chain(last)
                chain(nc.vector.bn_aggr(mv3[:, 0:2, b], st3[:, b, :, :].rearrange("p a b -> p (a b)")))

            def channel_squares(a, b):
                m = mv3[:, :, a:b]
                chain(nc.vector.tensor_tensor(m[:, 2, :], m[:, 0, :], m[:, 0, :], ALU.mult))
                nc.vector.tensor_tensor(m[:, 1, :], m[:, 1, :], m[:, 2, :], ALU.add).then_inc(gs_done, b - a)

            def group_norm3(a, b):
                m = mv3[:, :, a:b]
                dve.wait_ge(gm_done, b)
                chain(nc.vector.tensor_copy(m[:, 2:4, :], bank(4, 2 * (b - a)).rearrange("p (v b) -> p v b", v=2)))
                chain(nc.vector.tensor_tensor(m[:, 4, :], m[:, 2, :], m[:, 2, :], ALU.mult))
                nc.vector.scalar_tensor_tensor(m[:, 4, :], m[:, 3, :], GN_EPS, m[:, 4, :], ALU.add,
                                               ALU.subtract).then_inc(gn3v_done, b - a)
                dve.wait_ge(gn3s_done, 1 + (a > 0))
                chain(nc.vector.tensor_scalar(m[:, 7, :], m[:, 5, :], gn[:, 4:5], None, ALU.mult))
                chain(nc.vector.tensor_tensor(m[:, 8, :], m[:, 7, :], m[:, 2, :], ALU.mult))
                nc.vector.tensor_scalar(m[:, 8, :], m[:, 8, :], -1.0, gn[:, 5:6], ALU.mult,
                                        ALU.add).then_inc(gn3a_done, b - a)

            def residual(b):
                s = slice(b * HW, (b + 1) * HW)
                dve.wait_ge(r3_done, b + 1)
                nc.vector.tensor_tensor(X[:, s], X[:, s], R3[:, b, :], ALU.add).then_inc(x1_done[b], 1)

            def token_stats(b):
                s = slice(b * PT, (b + 1) * PT)
                for i in range(PT):
                    if i % 2 == 0:
                        dve.wait_ge(tokc_done, (b * PT + i) // 2 + 1)
                    last = nc.vector.bn_stats(st4[:, b * PT + i, :], XTL[:, b * PT + i, 0:C])
                chain(last)
                me, ve, mo, vo = (st4[:, s, k] for k in (1, 2, 4, 5))
                chain(nc.vector.tensor_tensor(ts[:, 0, s], me, mo, ALU.subtract))
                chain(nc.vector.tensor_tensor(ts[:, 0, s], ts[:, 0, s], ts[:, 0, s], ALU.mult))
                chain(nc.vector.tensor_tensor(ts[:, 1, s], ve, vo, ALU.add))
                chain(nc.vector.scalar_tensor_tensor(ts[:, 1, s], ts[:, 0, s], C / 4.0, ts[:, 1, s], ALU.mult, ALU.add))
                nc.vector.tensor_scalar(ts[:, 1, s], ts[:, 1, s], 1.0 / C, LN_T_EPS, ALU.mult,
                                        ALU.add).then_inc(tvar_done, 1)
                chain(nc.vector.tensor_tensor(ts[:, 2, s], me, mo, ALU.add))

            def token_norm(b):
                s = slice(b * PT, (b + 1) * PT)
                dve.wait_ge(tstd_done, b + 1)
                chain(nc.vector.tensor_scalar(rN[:, s], gw[:, 0, s], SN, None, ALU.mult))
                chain(nc.vector.scalar_tensor_tensor(nb[:, s], ts[:, 2, s], -0.5, rN[:, s], ALU.mult, ALU.mult))
                for i in range(PT):
                    t = b * PT + i
                    nc.vector.tensor_scalar(XN[:, b, i, :], XTL[:, t, 0:C], rN[:, t:t + 1], nb[:, t:t + 1], ALU.mult,
                                            ALU.add).then_inc(xn_done, 1)

            for b in range(3):
                channel_stats(b)
            channel_squares(0, 3)
            group_norm3(0, 3)
            residual(0)
            channel_stats(3)
            channel_squares(3, 4)
            residual(2)
            token_stats(0)
            group_norm3(3, 4)
            for b in range(1, B):
                token_norm(b - 1)
                token_stats(b)
            def te(v):
                return v.rearrange("p (t e) -> p t e", e=E)

            L, eq, code, oh1, oh2 = (te(g8[:, k, :]) for k in range(5))

            def choose(a, b):
                n = b - a
                i8 = prm_("iota8").unsqueeze(1).to_broadcast([P, n, E])

                def wide(v):
                    return v[:, a:b].unsqueeze(2).to_broadcast([P, n, E])

                chain(nc.vector.tensor_tensor(L[:, a:b, :], XTL[:, a:b, C:C + E], wide(gw[:, 0, :]), ALU.mult))

                def largest(top, first, onehot):
                    chain(nc.vector.tensor_reduce(top[:, a:b], L[:, a:b, :], AX_X, ALU.max))
                    chain(nc.vector.tensor_tensor(eq[:, a:b, :], L[:, a:b, :], wide(top), ALU.is_equal))
                    chain(nc.vector.scalar_tensor_tensor(code[:, a:b, :], eq[:, a:b, :], -float(E), i8, ALU.mult, ALU.add))
                    chain(nc.vector.tensor_reduce(first[:, a:b], code[:, a:b, :], AX_X, ALU.min))
                    chain(nc.vector.tensor_tensor(onehot[:, a:b, :], code[:, a:b, :], wide(first), ALU.is_equal))

                largest(gw[:, 1, :], gw[:, 6, :], oh1)
                chain(nc.vector.scalar_tensor_tensor(L[:, a:b, :], oh1[:, a:b, :], -1e30, L[:, a:b, :], ALU.mult, ALU.add))
                largest(gw[:, 5, :], gw[:, 6, :], oh2)

            choose(0, TT - PT)
            token_norm(B - 1)
            choose(TT - PT, TT)
            et = "p (e t) -> p t e"
            nc.vector.tensor_tensor(mask16[:, :].rearrange(et, e=E), oh1, oh2, ALU.add).then_inc(mask_done, 1)
            nc.vector.tensor_tensor(gw[:, 2, :], gw[:, 5, :], gw[:, 1, :], ALU.subtract).then_inc(gsub_done, 1)
            tot, inc, sl = g8[:, 5, :], g8[:, 6, :], g8[:, 7, :]
            dve.wait_ge(rank_done, 1)
            chain(nc.vector.tensor_copy(tot, bank(1, E * TT)))
            chain(nc.vector.tensor_tensor_scan(inc, tot, tot, 0.0, ALU.add, ALU.max))
            ends = inc.rearrange("p (e t) -> p e t", e=E)[:, :, TT - 1]
            begin, cnt, ntl, tend, off = (e8[:, k, :] for k in range(5))
            chain(nc.vector.memset(begin, 0.0))
            chain(nc.vector.tensor_copy(begin[:, 1:E], ends[:, 0:E - 1]))
            chain(nc.vector.tensor_tensor(cnt, ends, begin, ALU.subtract))
            chain(nc.vector.tensor_scalar(e8i[:, 0, :], cnt, float(P - 1), None, ALU.add))
            chain(nc.vector.tensor_scalar(e8i[:, 1, :], e8i[:, 0, :], 7, None, ALU.arith_shift_right))
            chain(nc.vector.tensor_copy(ntl, e8i[:, 1, :]))
            chain(nc.vector.tensor_tensor_scan(tend, ntl, ntl, 0.0, ALU.add, ALU.max))
            chain(nc.vector.tensor_tensor(off, tend, ntl, ALU.subtract))
            chain(nc.vector.scalar_tensor_tensor(off, off, float(P), begin, ALU.mult, ALU.subtract))
            chain(nc.vector.tensor_tensor(inc, inc, tot, ALU.subtract))
            by_e = lambda v: v.rearrange("p (e t) -> p e t", e=E)
            chain(nc.vector.tensor_tensor(by_e(inc), by_e(inc), off.unsqueeze(2).to_broadcast([P, E, TT]), ALU.add))
            chain(nc.vector.tensor_tensor(sl, inc, bank(0, E * TT), ALU.add))
            for c, oh in enumerate((oh1, oh2)):
                chain(nc.vector.tensor_tensor(code, oh, sl.rearrange(et, e=E), ALU.mult))
                chain(nc.vector.tensor_reduce(qr[:, 0, c * TT:(c + 1) * TT], code, AX_X, ALU.add))
            chain(nc.vector.tensor_copy(si[:, 0, :], qr[:, 0, :]))
            chain(nc.vector.tensor_scalar(si[:, 1, :], si[:, 0, :], 7, None, ALU.arith_shift_right))
            chain(nc.vector.tensor_scalar(si[:, 2, :], si[:, 0, :], P - 1, None, ALU.bitwise_and))
            nc.vector.tensor_copy(qr[:, 0, :], si[:, 1, :]).then_inc(qr_done, 1)
            chain(nc.vector.tensor_copy(qr[:, 1, :], si[:, 2, :]))
            dve.wait_ge(qr_done, 1)
            chain(nc.vector.tensor_copy(q16[:, :], qr[:, 0, :]))
            dve.wait_ge(lo_done, B)
            for n0 in range(0, 2 * TT, OHN):
                s = slice(n0, n0 + OHN)
                chain(nc.vector.tensor_tensor(OHQ[:, s, 1, :], k16_("iotaq").unsqueeze(1).to_broadcast([P, OHN, NQ]),
                                              q16[:, s].unsqueeze(2).to_broadcast([P, OHN, NQ]), ALU.is_equal))
                nc.vector.tensor_scalar(OHQ[:, s, 0, :], OHQ[:, s, 1, :], prm_("row1"), None,
                                        ALU.mult).then_inc(oh_done, 1)
                for n in range(n0, n0 + OHN):
                    nc.vector.tensor_scalar(OHR[:, n, :], k16_("iota"), qr[:, 1, n:n + 1], None,
                                            ALU.is_equal).then_inc(ohr_done, 1)
            gq = ge[:, :].rearrange("p (q e) -> p q e", e=E)
            chain(nc.vector.tensor_tensor(gq, prm_("iotaq").unsqueeze(2).to_broadcast([P, NQ, E]),
                                          tend.unsqueeze(1).to_broadcast([P, NQ, E]), ALU.is_ge))
            chain(nc.vector.tensor_reduce(eid[:, :], gq, AX_X, ALU.add))
            nc.vector.tensor_scalar(eidi[:, :], eid[:, :], float(E - 1), None, ALU.min).then_inc(eid_done, 1)
            dve.wait_ge(gexp_done, 1)
            chain(nc.vector.tensor_scalar(gw[:, 7, :], gw[:, 3, :], 1.0, None, ALU.add))
            chain(nc.vector.reciprocal(gw[:, 4, :], gw[:, 7, :]))
            nc.vector.tensor_tensor(gw[:, 8, :], gw[:, 4, :], gw[:, 3, :], ALU.mult).then_inc(gates_done, 1)
            dve.wait_ge(dest_done, 1)
            chain(nc.vector.tensor_copy(dst[:, 0:2, :].rearrange("p a q -> p (a q)"), bank(4, 2 * NQ)))
            chain(nc.vector.scalar_tensor_tensor(dst[:, 2, :], dst[:, 1, :], float(P), dst[:, 0, :], ALU.mult, ALU.add))
            chain(nc.vector.tensor_scalar(dst[:, 2, :], dst[:, 2, :], -1.0, None, ALU.add))
            chain(nc.vector.tensor_scalar(dsti[:, 0, :], dst[:, 2, :], 0.0, None, ALU.max))
            chain(nc.vector.tensor_scalar(dsti[:, 1, :], dsti[:, 0, :], T - 1, None, ALU.bitwise_and))
            chain(nc.vector.tensor_scalar(dst[:, 0, :], dst[:, 2, :], 0.0, 4.0 * T, ALU.is_lt, ALU.mult))
            chain(nc.vector.tensor_tensor(dsti[:, 2, :], dst[:, 0, :], dst[:, 2, :], ALU.add))
            for q in range(ILAG):
                nc.vector.tensor_copy(gidx[:, q:q + 1], dsti[:, 1, q:q + 1]).then_inc(gidx_ready, 1)

            def split(q, slot, lap):
                dve.wait_ge(gelu_done, q + 1)
                at_least(dve, y_done, q - 1)
                nc.vector.tensor_scalar(HS[:, slot % 2, 0, :], GF[:, slot % 2, :], SH, None, ALU.mult).then_inc(hs_done, 1)
                dve.wait_ge(hs_done, q + 1)
                nc.vector.scalar_tensor_tensor(HS[:, slot % 2, 1, :], GF[:, slot % 2, :], SH, HS[:, slot % 2, 0, :], ALU.mult,
                                               ALU.subtract).then_inc(split_done, 1)

            def finish(q, slot, lap):
                e = dve.value_load(eidi[0:1, bass.ds(q, 1)], min_val=0, max_val=E - 1)
                dve.wait_ge(y_done, q + 1)
                at_least(dve, ys_done, q - 1)
                nc.vector.scalar_tensor_tensor(YH[:, slot % 2, :], PS[:, 4 + slot % 2, C:2 * C], 1.0 / (SH * SW),
                                               B2[:, bass.ds(e * C, C)], ALU.mult, ALU.add).then_inc(yh_done, 1)
                at_least(dve, y_out[slot], 16 * lap)
                nc.vector.tensor_copy(sidx[:, slot:slot + 1], dsti[:, 2, bass.ds(q, 1)]).then_inc(yh_done, 1)
                dve.wait_ge(yh_done, 2 * (q + 1))
                nc.vector.scalar_tensor_tensor(YS[:, slot, :], PS[:, 4 + slot % 2, 0:C], 1.0 / (SH * SW), YH[:, slot % 2, :], ALU.mult,
                                               ALU.add).then_inc(ys_done, 1)

            def next_index(q, slot, lap):
                at_least(dve, g_in[slot], 16 * lap)
                nc.vector.tensor_copy(gidx[:, slot:slot + 1], dsti[:, 1, bass.ds(q, 1)]).then_inc(gidx_ready, 1)

            def step(i, j):
                if exists(tile(i, j, ILAG)[0]):
                    next_index(*tile(i, j, ILAG))
                if exists(tile(i, j)[0]):
                    split(*tile(i, j))
                if exists(tile(i, j, -1)[0]):
                    finish(*tile(i, j, -1))

            dve.wait_ge(b2_ready, 1)
            dve.wait_ge(eid_done, 1)
            run_steps(dve, step)
            for b in range(B + 1):
                if b < B:
                    for i in range(PT):
                        t = b * PT + i
                        dve.wait_ge(first_done, t + 1)
                        nc.vector.scalar_tensor_tensor(CMB[:, b % 2, i, :], YIN[:, 1, t, :], gw[:, 8, t:t + 1],
                                                       CMB[:, b % 2, i, :], ALU.mult, ALU.add).then_inc(comb_done, 1)
                if b >= 1:
                    c = b - 1
                    if c >= 2:
                        dve.wait_ge(out_done[c - 2], 16)
                    for h in range(2):
                        dve.wait_ge(ot_done, 2 * c + h + 1)
                        last = nc.vector.tensor_tensor(OUT[:, c % 2, h * HALF:(h + 1) * HALF], bank(2 * (c % 2) + h),
                                                       X[:, c * HW + h * HALF:c * HW + (h + 1) * HALF], ALU.add)
                    last.then_inc(fin_done, 1)

        @block.tensor
        def _(pe):
            pe.wait_ge(small_in, 16)
            nc.tensor.matmul(bank(7, CI + E), prm_("avg"), prm[:, COLS["w1"][0]:COLS["gate"][1]],
                             start=True, stop=True).then_inc(wmean_done, 1)

            def per_image(first_bank, lhs, rhs, done, wait=None):
                for h in range(2):
                    for b in range(B):
                        if wait:
                            wait(b)
                        last = nc.tensor.matmul(PS[b * CI:(b + 1) * CI, first_bank + h, :], lhs,
                                                rhs[:, b * HW + h * HALF:b * HW + (h + 1) * HALF], start=True, stop=True)
                    last.then_inc(done, 1)

            per_image(0, prm_("avg")[:, 0:CI], X, mean_done, lambda b: pe.wait_ge(x_in[b], 16))
            pe.wait_ge(wc_ready, 1)
            per_image(2, WC1[:, :], X, u_done)
            per_image(4, prm_("avg")[:, 0:CI], XSQ, msq_done, lambda b: pe.wait_ge(xsq_done, b + 1))

            def logits(d, tap):
                if tap == 0 and d >= 1:
                    pe.wait_ge(log_done, 2 * d)
                for m, t in enumerate((XH, XL)):
                    if d == 0 and tap == 0:
                        pe.wait_ge((xh_done, xl_done)[m], 1)
                    for h in range(2):
                        last = nc.tensor.matmul(PS[0:8 * KK, h, :], WCB[:, tap, d, :],
                                                tap_view(t, DILS[d], tap, h * RH, RH),
                                                start=(m == 0 and tap == 0), stop=(m == 1 and tap == KK - 1))
                if tap == KK - 1:
                    last.then_inc(logit_done, 1)

            def turn_logits(d):
                pe.wait_ge(log_done, 2 * (d + 1))
                if d >= 1:
                    pe.wait_ge(ftc_done, d)
                for i in range(PT):
                    last = nc.tensor.matmul(PS[:, 5, i * B * KK:(i + 1) * B * KK], LOG[0:8 * KK, d % 2, i * P:(i + 1) * P],
                                            prm_("fold")[0:8 * KK, :], start=True, stop=True)
                last.then_inc(tlog_done, 1)

            def turn_filters(d):
                pe.wait_ge(fhl_done, d + 1)
                w = 2 * B * KK
                for i in range(PT):
                    last = nc.tensor.transpose(PS[0:w, 5, i * (P // 2):(i + 1) * (P // 2)].bitcast(F16),
                                               FHL[:, d, :, :].rearrange("p a b -> p (a b)")[:, i * w:(i + 1) * w],
                                               k16_("ident"))
                last.then_inc(ft_done, 1)

            def spread(n):
                d, k = n // KK, n % KK
                if k == 0:
                    pe.wait_ge(ftc_done, d + 1)
                for h in range(2):
                    g = 2 * n + h
                    if g >= 3:
                        pe.wait_ge(prod_done, g - 2)
                    nc.tensor.matmul(bank(FB_BANK[g % 3]), k16_("sel")[0:8 * KK, k * P:(k + 1) * P],
                                     FT[0:8 * KK, d, h * HALF:(h + 1) * HALF], start=True, stop=True).then_inc(fb_done, 1)

            def accumulate(d):
                pe.wait_ge(sum2_done, d + 1)
                for h in range(2):
                    last = nc.tensor.matmul(bank(6 + h), W2B[:, 1 + d, :], SUM2[:, d % 2, h * HALF:(h + 1) * HALF],
                                            start=False, stop=(d == ND - 1))
                last.then_inc(acc_done, 1)

            pe.wait_ge(wcb_ready, 2 * B)
            for tap in range(KK):
                logits(0, tap)
            pe.wait_ge(c16_in, 16)
            turn_logits(0)
            for tap in range(FIRST_TAPS):
                logits(1, tap)
            turn_filters(0)
            pe.wait_ge(w2b_ready, 2 * B)
            pe.wait_ge(xd_done, 1)
            for h in range(2):
                last = nc.tensor.matmul(bank(6 + h), W2B[:, 0, :], tap_view(XD, 1, KK // 2, h * RH, RH),
                                        start=True, stop=False)
            last.then_inc(acc_done, 1)
            for n in range(NPR):
                spread(n)
                for d, tap in BESIDE[n]:
                    logits(d, tap)
                for d in range(1, ND):
                    if n == TOP_AT[d] - 1:
                        turn_logits(d)
                    if n == TOP_AT[d] + 2:
                        turn_filters(d)
                    if n == d * KK + ACC_AFTER:
                        accumulate(d - 1)
            accumulate(ND - 1)

            def third_conv(b):
                if b == 0:
                    pe.wait_ge(w3z_ready, B)
                    pe.wait_ge(y2_done, 1)
                    pe.wait_ge(prod_done, 2 * NPR)
                if b == 3:
                    pe.wait_ge(r3_done, 1)
                for h in range(2):
                    last = nc.tensor.matmul(bank(Y3_BANK[b] + h), W3Z[:, b, :], Y2[:, h * HALF:(h + 1) * HALF],
                                            start=True, stop=True)
                last.then_inc(y3_done, 1)

            def group_means(a, b):
                pe.wait_ge(gs_done, b)
                nc.tensor.matmul(bank(4, 2 * (b - a)), prm_("group"), mv3[:, 0:2, a:b],
                                 start=True, stop=True).then_inc(gm_done, b - a)

            def tokens(b):
                pe.wait_ge(x1_done[b], 1)
                for g in range(b * PT // 2, (b + 1) * PT // 2):
                    if g == 1:
                        pe.wait_ge(r3_done, 2)
                    if g >= 3:
                        pe.wait_ge(tokc_done, g - 2)
                    for i in range(2):
                        t = 2 * g + i
                        last = nc.tensor.matmul(PS[:, TOKEN_BANK[g % 3], i * (C + E):(i + 1) * (C + E)],
                                                X[:, t * P:(t + 1) * P], RG[:, :], start=True, stop=True)
                    last.then_inc(tok_done, 1)

            for b in range(3):
                third_conv(b)
            group_means(0, 3)
            third_conv(3)
            tokens(0)
            group_means(3, 4)
            for b in range(1, B):
                tokens(b)
            pe.wait_ge(mask_done, 1)
            nc.tensor.matmul(bank(0, E * TT), k16_("before"), mask16[:, :], start=True, stop=True)
            nc.tensor.matmul(bank(1, E * TT), k16_("ones"), mask16[:, :], start=True, stop=True).then_inc(rank_done, 1)
            for n in range(2 * TT):
                pe.wait_ge(ohr_done, n + 1)
                pe.wait_ge(ohq_done, n + 1)
                last = nc.tensor.matmul(bank(4, 2 * NQ), OHR[:, n, :], OHQ[:, n, :, :].rearrange("p v q -> p (v q)"),
                                        start=(n == 0), stop=(n == 2 * TT - 1))
            last.then_inc(dest_done, 1)
            pe.wait_ge(eid_done, 1)
            pe.wait_ge(wlo_done, 4)

            def turn(q, slot, lap):
                pe.wait_ge(g_in[slot], 16 * (lap + 1))
                at_least(pe, xtc_done, q - 1)
                for v in range(2):
                    last = nc.tensor.transpose(PS[:, slot % 2, v * (C // 2):(v + 1) * (C // 2)].bitcast(F16),
                                               GX[:, slot, v * C:(v + 1) * C], k16_("ident"))
                last.then_inc(xt_done, 1)

            def hidden(e, q, slot, lap):
                pe.wait_ge(xtc_done, q + 1)
                at_least(pe, gelu_done, q - 1)
                hi, lo = XT[:, slot % 2, 0:C], XT[:, slot % 2, C:2 * C]
                w = W1S[:, :, :, :].rearrange("p e v n -> p (e v n)")
                for c in range(HC):
                    o = PS[:, 2 + slot % 2, c * P:(c + 1) * P]
                    whi, wlo = (w[:, bass.ds(e * (2 * HID) + v * HID + c * P, P)] for v in range(2))
                    nc.tensor.matmul(o, whi, hi, start=True, stop=False)
                    nc.tensor.matmul(o, whi, lo, start=False, stop=False)
                    last = nc.tensor.matmul(o, wlo, hi, start=False, stop=True)
                last.then_inc(h_done, 1)

            def output(e, q, slot, lap):
                pe.wait_ge(split_done, q + 1)
                at_least(pe, ys_done, q - 1)
                w = W2S[:, :, :, :].rearrange("p e v n -> p (e v n)")
                for c in range(HC):
                    at = e * (2 * HID) + c * 2 * C

                    def low():
                        nc.tensor.matmul(PS[:, 4 + slot % 2, 0:C], HS[:, slot % 2, 1, c * P:(c + 1) * P],
                                         w[:, bass.ds(at, C)], start=False, stop=False)

                    if c:
                        low()
                    last = nc.tensor.matmul(PS[:, 4 + slot % 2, 0:2 * C], HS[:, slot % 2, 0, c * P:(c + 1) * P],
                                            w[:, bass.ds(at, 2 * C)], start=(c == 0), stop=(c == HC - 1))
                    if not c:
                        low()
                last.then_inc(y_done, 1)

            turn(*tile(0, 0))
            experts = {}

            def expert(q):
                return pe.value_load(eidi[0:1, bass.ds(q, 1)], min_val=0, max_val=E - 1)

            def step(i, j):
                if exists(tile(i, j, 1)[0]):
                    turn(*tile(i, j, 1))
                last_e = experts.pop("last", None)
                if exists(tile(i, j)[0]):
                    e = expert(tile(i, j)[0])
                    hidden(e, *tile(i, j))
                    if j < NR - 1:
                        experts["last"] = e
                if exists(tile(i, j, -1)[0]):
                    output(expert(tile(i, j, -1)[0]) if last_e is None else last_e, *tile(i, j, -1))

            run_steps(pe, step)
            for b in range(B):
                if b >= 2:
                    pe.wait_ge(fin_done, b - 1)
                for h in range(2):
                    pe.wait_ge(comb_done, b * PT + (h + 1) * PT // 2)
                    for i in range(PT // 2):
                        last = nc.tensor.transpose(PS[:, 2 * (b % 2) + h, i * P:(i + 1) * P],
                                                   CMB[:, b % 2, h * PT // 2 + i, :], prm_("ident"))
                    last.then_inc(ot_done, 1)


def kernel(**inputs):
    import concourse.bacc as _bacc
    from concourse.bass_utils import run_bass_kernel_spmd as _run

    a = {k.replace("L0_", ""): np.asarray(v) for k, v in inputs.items()}
    rep = lambda v: np.tile(v, (B, 1))
    col = lambda v, n: np.tile(v.reshape(-1, 1), (n, 1))
    wcat = np.stack([a[f"conv_w_cat{s}"].reshape(KK, CI, KK).transpose(1, 2, 0) for s in "abcd"], 2)
    c32, c16 = shape_constants()
    small = np.concatenate([
        col(a["conv_gn1_g"], B), col(a["conv_gn1_b"], B), col(a["conv_gn2_g"], B), col(a["conv_gn2_b"], B),
        col(a["conv_gn3_g"], 1), col(a["conv_gn3_b"], 1),
        a["ffn_b1"].reshape(E * HC, P).T,
        a["conv_w_scale1"].reshape(CI, C).T, a["ffn_gate_w"].T,
        rep(wcat.reshape(CI, -1)),
        rep(a["conv_w_scale2"].reshape(CI, 5, CI).transpose(2, 1, 0).reshape(CI, -1)),
        rep(a["conv_w_scale3"].reshape(C, CI).T),
        c32], 1)
    arrays = {
        "x": a["x"].reshape(B, C, HW), "small": small, "c16": c16,
        "w1t": a["ffn_w1"].transpose(2, 0, 1).reshape(P, E * HID),
        "w2t": a["ffn_w2"].reshape(E, C, HC, P).transpose(3, 0, 2, 1).reshape(P, E * HID),
        "b2": a["ffn_b2"].reshape(1, E * C),
    }
    arrays = {k: np.ascontiguousarray(v) for k, v in arrays.items()}
    nc = _bacc.Bacc("TRN2", target_bir_lowering=False, num_devices=1)
    aps = {k: nc.dram_tensor(k, v.shape, mybir.dt.from_np(v.dtype), kind="ExternalInput").ap() for k, v in arrays.items()}
    out = nc.dram_tensor("out", [B, C, HW], F32, kind="ExternalOutput").ap()
    build(nc, out=out, **aps)
    r = _run(nc, [arrays], core_ids=[0])
    return r.results[0]["out"].reshape(B, C, HH, WW)
```

```python
from contextlib import ExitStack

import concourse.bass as bass
import numpy as np
from concourse import mybir
from concourse.alu_op_type import AluOpType as ALU

ACT = mybir.ActivationFunctionType
F32 = mybir.dt.float32
F16 = mybir.dt.float16
I32 = mybir.dt.int32
U32 = mybir.dt.uint32
AX_X = mybir.AxisListType.X

P = 128
B, C, HH, WW = 4, 128, 32, 32
HW = HH * WW
T = B * HW
CI = 32
KK = 9
DILS = (1, 4, 8, 12)
ND = len(DILS)
PAD = max(DILS)
WP = HH + 2 * PAD
HALF = HW // 2
RH = HH // 2
PT = HW // P
TT = T // P
E, HID = 8, 512
HC = HID // P
NQ = (2 * T + E * (P - 1)) // P
LN_C_EPS, GN_EPS, LN_T_EPS = 1e-6, 1e-5, 1e-5

SX = 2.0 ** 7
SW = 2.0 ** 8
SF = 2.0 ** 12

COLS = {}


def _cols():
    at = 0
    for name, n in (("gn", 6), ("w1", CI), ("gate", E), ("wcat", KK * ND * KK), ("w2", 5 * CI),
                    ("w3", C), ("ident", P), ("avg", P), ("group", P), ("fold", 4 * KK), ("iota8", E),
                    ("iotaq", NQ), ("row1", 1)):
        COLS[name] = (at, at + n)
        at += n
    return at


NS = _cols()
WX = {"w1": (0, HID), "w2": (HID, 2 * HID), "b1": (2 * HID, 2 * HID + HC), "b2": (2 * HID + HC, 2 * HID + HC + C)}
NWX = WX["b2"][1]
C16 = {"ident": (0, P), "before": (P, 2 * P), "ones": (2 * P, 3 * P), "iota": (3 * P, 4 * P),
       "iotaq": (4 * P, 4 * P + NQ), "sel": (4 * P + NQ, 4 * P + NQ + KK * P)}
NC16 = C16["sel"][1]


def shape_constants():
    c32 = np.zeros((P, NS - COLS["ident"][0]), np.float32)
    base = COLS["ident"][0]

    def put(name, value, rows=P):
        a, b = COLS[name]
        c32[:rows, a - base:b - base] = value

    put("ident", np.eye(P))
    put("avg", 1.0 / C)
    put("group", np.kron(np.eye(C // 4), np.full((4, 4), 0.25)))
    fold = np.zeros((2, P // 2, B * KK))
    for pair in range(2):
        for w in range(2):
            fold[pair, 2 * KK * w:2 * KK * (w + 1), 2 * KK * pair:2 * KK * (pair + 1)] = np.eye(2 * KK)
    put("fold", fold.reshape(P, B * KK))
    put("iota8", np.arange(E))
    put("iotaq", np.arange(NQ))
    put("row1", np.arange(1, P + 1)[:, None])
    c16 = np.zeros((P, NC16), np.float16)
    c16[:, 0:P] = np.eye(P)
    c16[:, P:2 * P] = np.triu(np.ones((P, P)), 1)
    c16[:, 2 * P:3 * P] = 1.0
    c16[:, 3 * P:4 * P] = np.arange(P)
    c16[:, 4 * P:4 * P + NQ] = np.arange(NQ)
    sel = np.zeros((B, KK, 2, KK, B, CI), np.float16)
    for b in range(B):
        for k in range(KK):
            sel[b, k, :, k, b, :] = 1.0
    c16[:B * KK * 2, 4 * P + NQ:] = sel.reshape(B * KK * 2, KK * P)
    return c32, c16


def build(nc, x, small, c16, experts, out):
    ctx = ExitStack()
    with ctx:
        def sb(name, shape, dt=F32):
            return ctx.enter_context(nc.sbuf_tensor(name, shape, dt))

        def sem(name):
            return ctx.enter_context(nc.semaphore(name))

        X = sb("X", [P, T])
        prm = sb("prm", [P, NS])
        k16 = sb("k16", [P, NC16], F16)
        WALL = sb("WALL", [P, E, NWX])
        SCR = sb("SCR", [P, 2 * TT * C + NWX])
        RG = sb("RG", [P, P + E])
        WC1 = sb("WC1", [P, CI])
        WCS = sb("WCS", [P, 2, KK * ND * KK], F16)
        WCB = sb("WCB", [P, KK, ND, P // 2], F16)
        W2B = sb("W2B", [P, 5, P])
        W3Z = sb("W3Z", [P, B, P])
        MV = sb("MV", [P, 4, HW])
        MSQ, VAR, LOG = MV[:, 0, :], MV[:, 1, :], MV[:, 2:4, :]
        Z = sb("Z", [P, HW])
        RX = sb("RX", [P, 2 * WP * WP])
        XD = RX[:, 0:WP * WP].rearrange("p (h w) -> p h w", w=WP)
        XP = [RX[:, (2 + i) * WP * WP // 2:(3 + i) * WP * WP // 2].bitcast(F16).rearrange("p (h w) -> p h w", w=WP)
              for i in range(2)]
        HI = [slice(0, P // 2), slice(P // 2, P)]
        LO = HI[::-1]
        XTL = RX[:, 0:TT * (C + E)].rearrange("p (t n) -> p t n", t=TT)
        st = sb("st", [P, 2, 6])
        aff = sb("aff", [P, 16])
        FE = sb("FE", [P, 2, PT * B * KK])
        mx = sb("mx", [P, ND, PT * B])
        FHL = sb("FHL", [P, ND, PT * B * KK, 2], F16)
        FT = sb("FT", [P, ND, HW], F16)
        PR = sb("PR", [P, 8, HW])
        DIRECT = MV[:, 0:2, :]
        SUM1, SUM2, RING, OWN = PR[:, 0:2, :], PR[:, 2:4, :], PR[:, 4:7, :], PR[:, 7, :]
        R3 = PR[:, 0:4, :]
        NROW = C + 2
        XN = SCR[:, TT * C:TT * C + TT * NROW].rearrange("p (t n) -> p t n", n=NROW)
        XSQ = PR[:, 0:T // HW, :].rearrange("p a n -> p (a n)")
        Y2 = Z
        Y3_BANK = (0, 2, 6, 0)
        TOKEN_BANK = (5, 2, 3)
        OHN = 16
        OHR = SCR[:, 0:TT * C].bitcast(F16).rearrange("p (m r n) -> p m r n", r=P, n=OHN)
        OHQ = PR[:, :, :].rearrange("p a n -> p (a n)")[:, 0:3 * TT * NQ].bitcast(F16).rearrange(
            "p (m v q n) -> p m v q n", v=3, q=NQ, n=OHN)
        WIDE = RX[:, TT * (C + E):2 * WP * WP].bitcast(F16)
        IOTA_R = WIDE[:, 0:P * OHN].rearrange("p (r n) -> p r n", n=OHN)
        YIN = SCR[:, 0:2 * TT * C].rearrange("p (j t c) -> p j t c", j=2, c=C)
        CMB = PR[:, 0:2, :].rearrange("p s (i n) -> p s i n", n=C)
        OUT = PR[:, 2:4, :]
        st3 = sb("st3", [P, B, 2, 6])
        mv3 = sb("mv3", [P, 10, B])
        st4 = sb("st4", [P, TT, 6])
        ts = sb("ts", [P, 4, TT])
        gw = sb("gw", [P, 9, TT])
        rN, nb = gw[:, 0, :], ts[:, 3, :]
        g8 = FT[:, :, :].rearrange("p d n -> p (d n)").bitcast(F32).rearrange("p (k n) -> p k n", k=8)
        mask16 = sb("mask16", [P, E * TT], F16)
        e8 = sb("e8", [P, 3, E])
        e8i = sb("e8i", [P, 2, E], I32)
        si = sb("si", [P, 3, 2 * TT], I32)
        slot = sb("slot", [P, 2 * TT])
        q16, r16 = sb("q16", [P, 2 * TT], F16), sb("r16", [P, 2 * TT], F16)
        ge = FHL[:, :, :, :].rearrange("p d g v -> p (d g v)").bitcast(F32)[:, 0:NQ * E]
        eid = sb("eid", [P, NQ])
        eidi = sb("eidi", [P, NQ], I32)
        dst = sb("dst", [P, 2, NQ])
        chosen = sb("chosen", [P, 2, NQ])
        dsti = sb("dsti", [P, 3, NQ], I32)
        NR = 8
        gidx, sidx = sb("gidx", [P, NR], I32), sb("sidx", [P, NR], I32)
        WE = SCR[:, TT * C:TT * C + 4 * NWX].rearrange("p (s n) -> p s n", s=4)
        GX = PR[:, 6:8, :].rearrange("p s n -> p (s n)")[:, 0:NR * NROW].rearrange("p (r n) -> p r n", r=NR)
        gt = sb("gt", [P, 2, NR])
        XT = MV[:, 1, 0:4 * P].rearrange("p (s n) -> p s n", s=4)
        GF = MV[:, 0, :].rearrange("p (s n) -> p s n", s=2)
        YH = MV[:, 1, 4 * P:8 * P].rearrange("p (s n) -> p s n", s=4)
        YS = PR[:, 5, :].rearrange("p (r n) -> p r n", r=NR)
        PS = ctx.enter_context(nc.psum_tensor("PS", [P, 8, 512], F32))

        xr = nc.dram_tensor("token_rows", [T, NROW], F32).ap()
        yr = nc.dram_tensor("expert_rows", [2 * T, C], F32).ap()

        def prm_(name):
            a, b = COLS[name]
            return prm[:, a:b]

        def k16_(name):
            a, b = C16[name]
            return k16[:, a:b]

        def bank(i, n=512):
            return PS[:, i, 0:n]

        def banks2(i):
            return PS[:, i:i + 2, :].rearrange("p a n -> p (a n)")

        def tap_view(t, d, k, r0=0, rows=HH):
            oy, ox = PAD + d * (k // 3 - 1) + r0, PAD + d * (k % 3 - 1)
            return t[:, oy:oy + rows, ox:ox + WW]

        def plane(v):
            return v.rearrange("p (h w) -> p h w", w=WW)

        small_in, c16_in = sem("small_in"), sem("c16_in")
        w_in = [sem(f"w_in{w}") for w in range(2)]
        x_in = [sem(f"x_in{b}") for b in range(B)]
        wmean_done = sem("wmean_done")
        wc_ready = sem("wc_ready")
        wcb_ready, w2b_ready, w3z_ready = sem("wcb_ready"), sem("w2b_ready"), sem("w3z_ready")
        zero_done = sem("zero_done")
        xsq_done = sem("xsq_done")
        mean_done, u_done, msq_done = sem("mean_done"), sem("u_done"), sem("msq_done")
        mean2_done, var_done, std_done = sem("mean2_done"), sem("var_done"), sem("std_done")
        gvar_done, gstd_done, gaff_done = sem("gvar_done"), sem("gstd_done"), sem("gaff_done")
        xd_done, xh_done, xl_done = sem("xd_done"), sem("xh_done"), sem("xl_done")
        logit_done, log_done, tlog_done = sem("logit_done"), sem("log_done"), sem("tlog_done")
        fsub_done, fexp_done, fhl_done = sem("fsub_done"), sem("fexp_done"), sem("fhl_done")
        fmax_done, fsum_done, frec_done, fn_done, fhi_done = (sem(n) for n in (
            "fmax_done", "fsum_done", "frec_done", "fn_done", "fhi_done"))
        ft_done, ftc_done = sem("ft_done"), sem("ftc_done")
        fb_done, prod_done, acc_done = sem("fb_done"), sem("prod_done"), sem("acc_done")
        ring_used, own_used = sem("ring_used"), sem("own_used")
        oh_done, ohp_done, wide_done, gscale_done = sem("oh_done"), sem("ohp_done"), sem("wide_done"), sem("gscale_done")
        ln_done = sem("ln_done")
        gn2v_done, gn2s_done, gn2a_done, y2_done = sem("gn2v_done"), sem("gn2s_done"), sem("gn2a_done"), sem("y2_done")
        y3_done, gs_done, gm_done = sem("y3_done"), sem("gs_done"), sem("gm_done")
        gn3v_done, gn3s_done, gn3a_done = sem("gn3v_done"), sem("gn3s_done"), sem("gn3a_done")
        r3_done, x1_done = sem("r3_done"), [sem(f"x1_done{b}") for b in range(B)]
        tok_done, tokc_done = sem("tok_done"), sem("tokc_done")
        tstat_done, tvar_done, tstd_done, taff_done = sem("tstat_done"), sem("tvar_done"), sem("tstd_done"), sem("taff_done")
        xn_done, rows_out = sem("xn_done"), [sem(f"rows_out{b}") for b in range(B)]
        gsub_done, gexp_done = sem("gsub_done"), sem("gexp_done")
        mask_done, rank_done = sem("mask_done"), sem("rank_done")
        chosen_done, finish_step = sem("chosen_done"), sem("finish_step")
        zeros_done, si_done = sem("zeros_done"), sem("si_done")
        qr_done, ohr_done, ohq_done = sem("qr_done"), sem("ohr_done"), sem("ohq_done")
        dest_done, eid_done = sem("dest_done"), sem("eid_done")
        we_ready = sem("we_ready")
        gidx_ready = sem("gidx_ready")
        g_in = [sem(f"g_in{j}") for j in range(8)]
        y_out = [sem(f"y_out{j}") for j in range(8)]
        xt_done, xtc_done, h_done, gelu_done = sem("xt_done"), sem("xtc_done"), sem("h_done"), sem("gelu_done")
        y_done, ys_done = sem("y_done"), sem("ys_done")
        y_in = [sem(f"y_in{i}") for i in range(2 * B)]
        comb_done, ot_done, fin_done = sem("comb_done"), sem("ot_done"), sem("fin_done")
        gates_done = sem("gates_done")
        dve_step, pool_step = sem("dve_step"), sem("pool_step")
        out_done = [sem(f"out_done{b}") for b in range(B)]
        pool_held = sem("pool_held")

        PLAN = ('SsDssEsss', 'SsDssEsss', 'SsDssEsss', 'SPsPsDsPE')
        NPR = ND * KK

        def of_kind(kinds, n):
            return sum(1 for m in range(n) if PLAN[m // KK][m % KK] in kinds)

        FB_BANK = (2, 3, 4)

        def product_buffer(n):
            d, kind = n // KK, PLAN[n // KK][n % KK]
            return {"S": SUM2[:, d % 2, :], "D": SUM1[:, d % 2, :], "E": OWN, "s": RING[:, of_kind("s", n) % 3, :],
                    "P": DIRECT[:, of_kind("P", n) % 2, :]}[kind]

        TOP = 3
        SOFTMAX_STEPS = (0, 1, 2, 3, 4, 6)
        FILTERS_AT = 2 * TOP + 8
        LOGITS_AT = (8, 9, 9, 10, 11, 12, 12, 13, 14)
        FIRST_FILTERS_AFTER = 5
        ACCUMULATE = []
        for n in range(NPR):
            d, kind = n // KK, PLAN[n // KK][n % KK]
            for h in range(2):
                if kind == "E":
                    ACCUMULATE.append((2 * n + 7 + h, d, "D", h))
                if kind == "P":
                    ACCUMULATE.append((2 * n + 3 + h, d, n, h))
                if n % KK == KK - 1:
                    ACCUMULATE.append((2 * n + h + (14 if d < ND - 1 else 4), d, "S", h))
        ACCUMULATE.sort(key=lambda a: a[0])

        def accumulated(d, what):
            return 2 + [a[1:] for a in ACCUMULATE].index((d, what, 1))

        GLAG = 2
        TLEAD, OLAG = 2, 1
        WLEAD = 2
        SLAG = 7
        ILAG = 6
        NSTEP = NQ + GLAG

        def run_steps(engine, step):
            laps = (NQ - ILAG) // NR
            for s in range(2 * NR):
                step(s // NR, s % NR)
            with engine.Fori(2, laps) as i:
                for j in range(NR):
                    step(i, j)
            for s in range(NR * laps, NSTEP):
                step(s // NR, s % NR)

        def tile(i, j, ahead=0):
            return NR * i + (j + ahead), (j + ahead) % NR, i + (j + ahead) // NR

        def exists(q):
            return not isinstance(q, int) or 0 <= q < NQ

        def part(q_slot, name):
            a, b = WX[name]
            return WE[:, q_slot % 4, a:b]

        def at_least(engine, signal, value):
            if not isinstance(value, int) or value > 0:
                engine.wait_ge(signal, value)

        block = ctx.enter_context(nc.Block())

        @block.sync
        def _(sp):
            sp.dma_start(prm[:, :], small).then_inc(small_in, 16)
            for b in (1, 3):
                sp.dma_start(X[:, b * HW:(b + 1) * HW], x[b]).then_inc(x_in[b], 16)
            sp.dma_start(WALL[:, 0:E // 2, :], experts[:, 0:E // 2, :]).then_inc(w_in[0], 16)
            for b in range(B):
                sp.wait_ge(xn_done, PT * (b + 1))
                if b == 0:
                    sp.wait_ge(gates_done, 2)
                sp.dma_start(xr[b * HW:(b + 1) * HW, :].rearrange("(i p) n -> p i n", p=P),
                             XN[:, b * PT:(b + 1) * PT, :]).then_inc(rows_out[b], 16)
            for j in range(NR):
                sp.wait_ge(y_out[j], 16 * ((NQ - 1 - j) // NR + 1))
            for b in range(B):
                for h in range(2):
                    t0 = b * PT + h * PT // 2
                    for c in range(2):
                        sp.dma_start(YIN[:, c, t0:t0 + PT // 2, :], yr[c * T + t0 * P:c * T + t0 * P + HALF, :].rearrange(
                            "(i p) n -> p i n", p=P)).then_inc(y_in[2 * b + h], 16)
            for b in range(B):
                for h in range(2):
                    sp.wait_ge(fin_done, 2 * b + h + 1)
                    sp.dma_start(out[b][:, h * HALF:(h + 1) * HALF],
                                 OUT[:, b % 2, h * HALF:(h + 1) * HALF]).then_inc(out_done[b], 16)
            for b in range(B):
                sp.wait_ge(out_done[b], 32)

        @block.gpsimd
        def _(pool):
            for t in (XD, XP[0], XP[1], WCB, W2B, W3Z):
                ap = t[:, :, :] if len(t.shape) == 3 else t[:, :, :, :].rearrange("p a b c -> p a (b c)")
                nc.gpsimd.memset(ap, 0.0).then_inc(zero_done, 1)
            for d in range(ND):
                for n in range(d * KK, (d + 1) * KK):
                    if PLAN[d][n % KK] == "s":
                        pool.wait_ge(prod_done, 2 * n + 2)
                        if of_kind("s", n) > of_kind("s", d * KK):
                            pool.wait_ge(ring_used, of_kind("s", n))
                        nc.gpsimd.tensor_tensor(SUM2[:, d % 2, :], SUM2[:, d % 2, :], product_buffer(n),
                                                ALU.add).then_inc(ring_used, 1)
            steps = [0]

            def chain(ins):
                steps[0] += 1
                ins.then_inc(pool_step, 1)
                pool.wait_ge(pool_step, steps[0])

            def token_variance(b):
                s = slice(b * PT, (b + 1) * PT)
                me, ve, mo, vo = (st4[:, s, k] for k in (1, 2, 4, 5))
                pool.wait_ge(tstat_done, b + 1)
                chain(nc.gpsimd.tensor_tensor(ts[:, 0, s], me, mo, ALU.subtract))
                chain(nc.gpsimd.tensor_tensor(ts[:, 0, s], ts[:, 0, s], ts[:, 0, s], ALU.mult))
                chain(nc.gpsimd.tensor_scalar(ts[:, 0, s], ts[:, 0, s], C / 4.0, None, ALU.mult))
                chain(nc.gpsimd.tensor_tensor(ts[:, 1, s], ve, vo, ALU.add))
                chain(nc.gpsimd.tensor_tensor(ts[:, 1, s], ts[:, 1, s], ts[:, 0, s], ALU.add))
                nc.gpsimd.tensor_scalar(ts[:, 1, s], ts[:, 1, s], 1.0 / C, LN_T_EPS, ALU.mult,
                                        ALU.add).then_inc(tvar_done, 1)
                chain(nc.gpsimd.tensor_tensor(ts[:, 2, s], me, mo, ALU.add))
                chain(nc.gpsimd.tensor_scalar(ts[:, 2, s], ts[:, 2, s], -0.5, None, ALU.mult))
                pool.wait_ge(tstd_done, b + 1)
                nc.gpsimd.tensor_tensor(nb[:, s], ts[:, 2, s], rN[:, s], ALU.mult).then_inc(taff_done, 1)

            pool.wait_ge(logit_done, ND)
            nc.gpsimd.tensor_copy(IOTA_R, k16_("iota").unsqueeze(2).to_broadcast([P, P, OHN])).then_inc(wide_done, 1)
            s = slice(HW, 2 * HW)
            pool.wait_ge(r3_done, 2)
            nc.gpsimd.tensor_tensor(X[:, s], X[:, s], R3[:, 1, :], ALU.add).then_inc(x1_done[1], 1)
            for b in range(B):
                token_variance(b)
            pool.wait_ge(gsub_done, 1)
            nc.gpsimd.tensor_tensor(gw[:, 2, :], gw[:, 2, :], rN, ALU.mult).then_inc(gscale_done, 1)
            pool.wait_ge(gexp_done, 1)
            nc.gpsimd.tensor_scalar(gw[:, 4, :], gw[:, 3, :], 1.0, None, ALU.add).then_inc(gscale_done, 1)
            pool.wait_ge(gates_done, 1)
            nc.gpsimd.tensor_tensor(XN[:, :, C + 1], gw[:, 3, :], XN[:, :, C], ALU.mult).then_inc(gates_done, 1)
            for b in range(B):
                pool.wait_ge(rows_out[b], 16)

            def gather(q, slot, lap):
                pool.wait_ge(gidx_ready, q + 1)
                pool.sem_inc(pool_held, 1)
                nc.gpsimd.indirect_dma_start(GX[:, slot, :], None, xr, bass.IndirectOffsetOnAxis(
                    ap=gidx[:, slot:slot + 1].bitcast(U32), axis=0)).then_inc(g_in[slot], 16)

            def scatter(q, slot, lap):
                pool.wait_ge(ys_done, q + 1)
                pool.sem_inc(pool_held, 1)
                nc.gpsimd.indirect_dma_start(yr, bass.IndirectOffsetOnAxis(ap=sidx[:, slot:slot + 1].bitcast(U32), axis=0),
                                             YS[:, slot, :], None, bounds_check=2 * T - 1,
                                             oob_is_err=False).then_inc(y_out[slot], 16)

            def step(i, j):
                if exists(tile(i, j)[0]):
                    gather(*tile(i, j))
                if exists(tile(i, j, -SLAG)[0]):
                    scatter(*tile(i, j, -SLAG))

            run_steps(pool, step)
            for q in range(NSTEP - SLAG, NQ):
                scatter(q, q % NR, q // NR)

        @block.scalar
        def _(act):
            steps = [0]

            def inverse_std(out_, var, done):
                steps[0] += 1
                nc.scalar.activation(out_, var, ACT.Ln).then_inc(ln_done, 1)
                act.wait_ge(ln_done, steps[0])
                nc.scalar.activation(out_, out_, ACT.Exp, scale=-0.5).then_inc(done, 1)

            nc.scalar.preload_act_table_set("natural_log_exp_and_others")
            for b in (0, 2):
                act.dma_start(X[:, b * HW:(b + 1) * HW], x[b]).then_inc(x_in[b], 16)
            act.dma_start(k16[:, :], c16).then_inc(c16_in, 16)
            act.dma_start(WALL[:, E // 2:E, :], experts[:, E // 2:E, :]).then_inc(w_in[1], 16)
            for b in range(B):
                act.wait_ge(x_in[b], 16)
                nc.scalar.activation(XSQ[:, b * HW:(b + 1) * HW], X[:, b * HW:(b + 1) * HW],
                                     ACT.Square).then_inc(xsq_done, 1)
            for h in range(2):
                act.wait_ge(mean_done, h + 1)
                nc.scalar.activation(MSQ[:, h * HALF:(h + 1) * HALF], bank(h), ACT.Square).then_inc(mean2_done, 1)
            for h in range(2):
                act.wait_ge(var_done, h + 1)
                inverse_std(MSQ[:, h * HALF:(h + 1) * HALF], VAR[:, h * HALF:(h + 1) * HALF], std_done)
            act.wait_ge(gvar_done, 1)
            inverse_std(aff[:, 3:4], aff[:, 1:2], gstd_done)
            act.wait_ge(gaff_done, 1)
            act.wait_ge(zero_done, 3)
            inner = (slice(PAD, PAD + HH), slice(PAD, PAD + WW))
            nc.scalar.activation(XD[(slice(None),) + inner], plane(Z[:, :]), ACT.Relu,
                                 bias=aff[:, 5:6], scale=aff[:, 4:5]).then_inc(xd_done, 1)
            r = HI[1]
            nc.scalar.activation(XP[1][(r,) + inner], plane(Z[r, :]), ACT.Relu,
                                 bias=aff[r, 7:8], scale=aff[r, 6:7]).then_inc(xh_done, 1)

            def evacuate_logits(d):
                act.wait_ge(logit_done, d + 1)
                if d >= 2:
                    act.wait_ge(tlog_done, d - 1)
                for h in range(2):
                    nc.scalar.activation(LOG[:, d % 2, h * HALF:(h + 1) * HALF], PS[:, h, :],
                                         ACT.Copy, scale=1.0 / (SX * SW)).then_inc(log_done, 1)

            def exponential(d):
                act.wait_ge(fsub_done, d + 1)
                nc.scalar.activation(FE[:, d % 2, :], FE[:, d % 2, :], ACT.Exp).then_inc(fexp_done, 1)
                act.wait_ge(fn_done, d + 1)
                nc.scalar.activation(FHL[:, d, :, 0], FE[:, d % 2, :], ACT.Copy).then_inc(fhi_done, 1)

            def evacuate_filters(d):
                act.wait_ge(ft_done, d + 1)
                nc.scalar.activation(FT[0:8 * KK, d, :], PS[0:8 * KK, 5, :].bitcast(F16), ACT.Copy).then_inc(ftc_done, 1)

            for d in range(ND):
                evacuate_logits(d)
                exponential(d)
                evacuate_filters(d)
            act.wait_ge(gn2v_done, 1)
            inverse_std(aff[:, 3:4], aff[:, 1:2], gn2s_done)
            act.wait_ge(gn2a_done, 1)
            nc.scalar.activation(Y2[:, :], banks2(6), ACT.Relu, bias=aff[:, 5:6], scale=aff[:, 4:5]).then_inc(y2_done, 1)

            def relu3(images):
                part = slice(images[0], images[-1] + 1)
                act.wait_ge(gn3v_done, images[-1] + 1)
                inverse_std(mv3[:, 5, part], mv3[:, 4, part], gn3s_done)
                act.wait_ge(gn3a_done, images[-1] + 1)
                for b in images:
                    nc.scalar.activation(R3[:, b, :], banks2(Y3_BANK[b]), ACT.Relu,
                                         bias=mv3[:, 8, b:b + 1], scale=mv3[:, 7, b:b + 1]).then_inc(r3_done, 1)

            def evacuate_tokens(b, groups=range(PT // 2)):
                for g in (b * PT // 2 + i for i in groups):
                    act.wait_ge(tok_done, g + 1)
                    nc.scalar.activation(XTL[:, 2 * g:2 * g + 2, :].rearrange("p a n -> p (a n)"),
                                         PS[:, TOKEN_BANK[g % 3], 0:2 * (C + E)], ACT.Copy).then_inc(tokc_done, 1)

            def token_scale(b):
                act.wait_ge(tvar_done, b + 1)
                inverse_std(gw[:, 0, b * PT:(b + 1) * PT], ts[:, 1, b * PT:(b + 1) * PT], tstd_done)

            def token_norm(b, tiles=range(PT)):
                act.wait_ge(taff_done, b + 1)
                for t in (b * PT + i for i in tiles):
                    nc.scalar.activation(XN[:, t, 0:C], XTL[:, t, 0:C], ACT.Identity, bias=nb[:, t:t + 1],
                                         scale=rN[:, t:t + 1]).then_inc(xn_done, 1)

            relu3((0, 1, 2))
            evacuate_tokens(0)
            relu3((3,))
            evacuate_tokens(1)
            token_scale(0)
            evacuate_tokens(2)
            for i in range(PT // 2):
                evacuate_tokens(3, (i,))
                token_norm(0, (2 * i, 2 * i + 1))
            for b in range(1, B):
                token_scale(b)
                token_norm(b)
            act.wait_ge(gscale_done, 1)
            nc.scalar.activation(gw[:, 3, :], gw[:, 2, :], ACT.Exp).then_inc(gexp_done, 1)
            act.wait_ge(gscale_done, 2)
            nc.scalar.activation(gw[:, 4, :], gw[:, 4, :], ACT.Ln).then_inc(gexp_done, 1)
            act.wait_ge(gexp_done, 2)
            nc.scalar.activation(XN[:, :, C], gw[:, 4, :], ACT.Exp, scale=-1.0).then_inc(gates_done, 1)
            for m in range(2 * TT // OHN):
                act.wait_ge(oh_done, m + 1)
                nc.scalar.activation(OHQ[:, m, 1, :, :], OHQ[:, m, 2, :, :], ACT.Copy, scale=prm_("row1")).then_inc(ohp_done, 1)
            nc.scalar.preload_act_table_set("gelu_and_others")

            def turned(q, slot, lap):
                act.wait_ge(xt_done, q + 1)
                nc.scalar.activation(XT[:, slot % 4, :], PS[:, slot % 2, 0:P], ACT.Copy).then_inc(xtc_done, 1)

            def gelu(q, slot, lap):
                act.wait_ge(h_done, q + 1)
                for c in range(HC):
                    last = nc.scalar.activation(GF[:, slot % 2, c * P:(c + 1) * P], PS[:, 2 + slot % 2, c * P:(c + 1) * P],
                                                ACT.Gelu, bias=part(slot, "b1")[:, c:c + 1])
                last.then_inc(gelu_done, 1)

            def apply_gate(q, slot, lap):
                act.wait_ge(finish_step, 3 * (q + 1))
                nc.scalar.activation(YS[:, slot, :], YH[:, slot % 4, :], ACT.Copy,
                                     scale=gt[:, 1, slot:slot + 1]).then_inc(ys_done, 1)

            for q in range(TLEAD):
                turned(*tile(0, q))

            def step(i, j):
                if exists(tile(i, j)[0]):
                    gelu(*tile(i, j))
                if exists(tile(i, j, TLEAD)[0]):
                    turned(*tile(i, j, TLEAD))
                if exists(tile(i, j, -GLAG)[0]):
                    apply_gate(*tile(i, j, -GLAG))

            run_steps(act, step)
        @block.vector
        def _(dve):
            steps = [0]

            def chain(ins):
                steps[0] += 1
                ins.then_inc(dve_step, 1)
                dve.wait_ge(dve_step, steps[0])

            dve.wait_ge(small_in, 16)
            a, g = COLS["w1"][0], COLS["gate"][0]
            nc.vector.tensor_copy(RG[:, 0:P], prm_("ident"))
            dve.wait_ge(wmean_done, 1)
            nc.vector.tensor_tensor(WC1[:, :], prm_("w1"), bank(7, CI), ALU.subtract).then_inc(wc_ready, 1)
            nc.vector.tensor_tensor(RG[:, P:P + E], prm_("gate"), PS[:, 7, CI:CI + E], ALU.subtract).then_inc(wc_ready, 1)
            chain(nc.vector.tensor_scalar(WCS[:, 0, :], prm_("wcat"), SW, None, ALU.mult))
            chain(nc.vector.scalar_tensor_tensor(WCS[:, 1, :], prm_("wcat"), SW, WCS[:, 0, :], ALU.mult, ALU.subtract))
            dve.wait_ge(zero_done, 6)
            for b in range(B):
                rows = slice(b * CI, (b + 1) * CI)
                for s in range(2):
                    o = 2 * KK * s + KK * (b % 2)
                    nc.vector.tensor_copy(WCB[rows, :, :, o:o + KK], WCS[rows, s, :].rearrange(
                        "p (t d k) -> p t d k", t=KK, d=ND)).then_inc(wcb_ready, 1)
                w2 = prm_("w2").rearrange("p (s o) -> p s o", s=5)
                nc.vector.tensor_copy(W2B[rows, 0, b * CI:(b + 1) * CI], w2[rows, 0, :]).then_inc(w2b_ready, 1)
                nc.vector.tensor_scalar(W2B[rows, 1:5, b * CI:(b + 1) * CI], w2[rows, 1:5, :], 1.0 / SF, None,
                                        ALU.mult).then_inc(w2b_ready, 1)
                nc.vector.tensor_copy(W3Z[rows, b, :], prm_("w3")[rows, :]).then_inc(w3z_ready, 1)
            for h in range(2):
                s = slice(h * HALF, (h + 1) * HALF)
                dve.wait_ge(mean2_done, h + 1)
                dve.wait_ge(msq_done, h + 1)
                nc.vector.scalar_tensor_tensor(VAR[:, s], bank(4 + h), LN_C_EPS, MSQ[:, s], ALU.add,
                                               ALU.subtract).then_inc(var_done, 1)
            for h in range(2):
                s = slice(h * HALF, (h + 1) * HALF)
                dve.wait_ge(std_done, h + 1)
                dve.wait_ge(u_done, h + 1)
                chain(nc.vector.tensor_tensor(Z[:, s], bank(2 + h), MSQ[:, s], ALU.mult))
                chain(nc.vector.bn_stats(st[:, h, :], Z[:, s]))
            gn = prm_("gn")
            chain(nc.vector.bn_aggr(aff[:, 0:2], st[:, :, :].rearrange("p a b -> p (a b)")))
            nc.vector.tensor_scalar(aff[:, 1:2], aff[:, 1:2], GN_EPS, None, ALU.add).then_inc(gvar_done, 1)
            dve.wait_ge(gstd_done, 1)
            chain(nc.vector.tensor_tensor(aff[:, 4:5], aff[:, 3:4], gn[:, 0:1], ALU.mult))
            chain(nc.vector.tensor_tensor(aff[:, 5:6], aff[:, 4:5], aff[:, 0:1], ALU.mult))
            chain(nc.vector.tensor_tensor(aff[:, 5:6], gn[:, 1:2], aff[:, 5:6], ALU.subtract))
            nc.vector.tensor_scalar(aff[:, 6:8], aff[:, 4:6], SX, None, ALU.mult).then_inc(gaff_done, 1)
            dve.wait_ge(xd_done, 1)
            inner = (slice(PAD, PAD + HH), slice(PAD, PAD + WW))
            chain(nc.vector.tensor_scalar(XP[0][(HI[0],) + inner], XD[(HI[0],) + inner], SX, None, ALU.mult))
            for i in range(2):
                if i == 1:
                    dve.wait_ge(xh_done, 1)
                r = (HI[i],) + inner
                nc.vector.scalar_tensor_tensor(XP[i][(LO[i],) + inner], XD[r], SX, XP[i][r], ALU.mult,
                                               ALU.subtract).then_inc(xl_done, 1)

            def softmax(d, step):
                tl = PS[:, 5, 0:PT * B * KK].rearrange("p (g k) -> p g k", k=KK)
                fe = FE[:, d % 2, :].rearrange("p (g k) -> p g k", k=KK)
                m, wide = mx[:, d, :], mx[:, d, :].unsqueeze(2).to_broadcast([P, PT * B, KK])
                if step == 0:
                    dve.wait_ge(tlog_done, d + 1)
                    nc.vector.tensor_reduce(m, tl, AX_X, ALU.max).then_inc(fmax_done, 1)
                if step == 1:
                    dve.wait_ge(fmax_done, d + 1)
                    nc.vector.tensor_tensor(fe, tl, wide, ALU.subtract).then_inc(fsub_done, 1)
                if step == 2:
                    dve.wait_ge(fexp_done, d + 1)
                    nc.vector.tensor_reduce(m, fe, AX_X, ALU.add).then_inc(fsum_done, 1)
                if step == 3:
                    dve.wait_ge(fsum_done, d + 1)
                    nc.vector.reciprocal(m, m).then_inc(frec_done, 1)
                if step == 4:
                    dve.wait_ge(frec_done, d + 1)
                    nc.vector.scalar_tensor_tensor(fe, fe, SF, wide, ALU.mult, ALU.mult).then_inc(fn_done, 1)
                if step == 5:
                    dve.wait_ge(fhi_done, d + 1)
                    nc.vector.tensor_tensor(FHL[:, d, :, 1], FE[:, d % 2, :], FHL[:, d, :, 0], ALU.subtract).then_inc(fhl_done, 1)

            for step in range(6):
                softmax(0, step)
            for n in range(NPR):
                d, k = n // KK, n % KK
                buffer = product_buffer(n)
                kind = PLAN[d][k]
                if kind in "SD" and d >= 2:
                    dve.wait_ge(acc_done, accumulated(d - 2, kind))
                if kind == "P" and of_kind("P", n) >= 2:
                    dve.wait_ge(acc_done, accumulated(*[(m // KK, m) for m in range(n) if PLAN[m // KK][m % KK] == "P"][-2]))
                if kind == "s" and of_kind("s", n) >= 3:
                    dve.wait_ge(ring_used, of_kind("s", n) - 2)
                if kind == "E" and d >= 1:
                    dve.wait_ge(own_used, d)
                for h in range(2):
                    if d + 1 < ND and 2 * k + h - 2 * TOP in SOFTMAX_STEPS:
                        softmax(d + 1, SOFTMAX_STEPS.index(2 * k + h - 2 * TOP))
                    dve.wait_ge(fb_done, 2 * n + h + 1)
                    nc.vector.tensor_tensor(plane(buffer[:, h * HALF:(h + 1) * HALF]),
                                            tap_view(XD, DILS[d], k, h * RH, RH),
                                            plane(bank(FB_BANK[(2 * n + h) % 3])), ALU.mult).then_inc(prod_done, 1)
                if kind == "E":
                    dve.wait_ge(prod_done, 2 * n + 2)
                    nc.vector.tensor_tensor(SUM1[:, d % 2, :], SUM1[:, d % 2, :], OWN, ALU.add).then_inc(own_used, 1)

            dve.wait_ge(acc_done, 1 + len(ACCUMULATE))
            for h in range(2):
                chain(nc.vector.bn_stats(st[:, h, :], bank(6 + h)))
            chain(nc.vector.bn_aggr(aff[:, 0:2], st[:, :, :].rearrange("p a b -> p (a b)")))
            nc.vector.tensor_scalar(aff[:, 1:2], aff[:, 1:2], GN_EPS, None, ALU.add).then_inc(gn2v_done, 1)
            dve.wait_ge(gn2s_done, 1)
            chain(nc.vector.tensor_tensor(aff[:, 4:5], aff[:, 3:4], gn[:, 2:3], ALU.mult))
            chain(nc.vector.tensor_tensor(aff[:, 5:6], aff[:, 4:5], aff[:, 0:1], ALU.mult))
            nc.vector.tensor_tensor(aff[:, 5:6], gn[:, 3:4], aff[:, 5:6], ALU.subtract).then_inc(gn2a_done, 1)

            def channel_stats(b):
                dve.wait_ge(y3_done, b + 1)
                for h in range(2):
                    last = nc.vector.bn_stats(st3[:, b, h, :], bank(Y3_BANK[b] + h))
                chain(last)
                chain(nc.vector.bn_aggr(mv3[:, 0:2, b], st3[:, b, :, :].rearrange("p a b -> p (a b)")))

            def channel_squares(a, b):
                m = mv3[:, :, a:b]
                chain(nc.vector.tensor_tensor(m[:, 2, :], m[:, 0, :], m[:, 0, :], ALU.mult))
                nc.vector.tensor_tensor(m[:, 1, :], m[:, 1, :], m[:, 2, :], ALU.add).then_inc(gs_done, b - a)

            def group_norm3(a, b):
                m = mv3[:, :, a:b]
                dve.wait_ge(gm_done, b)
                chain(nc.vector.tensor_copy(m[:, 2:4, :], bank(4, 2 * (b - a)).rearrange("p (v b) -> p v b", v=2)))
                chain(nc.vector.tensor_tensor(m[:, 4, :], m[:, 2, :], m[:, 2, :], ALU.mult))
                nc.vector.scalar_tensor_tensor(m[:, 4, :], m[:, 3, :], GN_EPS, m[:, 4, :], ALU.add,
                                               ALU.subtract).then_inc(gn3v_done, b - a)
                dve.wait_ge(gn3s_done, 1 + (a > 0))
                chain(nc.vector.tensor_scalar(m[:, 7, :], m[:, 5, :], gn[:, 4:5], None, ALU.mult))
                chain(nc.vector.tensor_tensor(m[:, 8, :], m[:, 7, :], m[:, 2, :], ALU.mult))
                nc.vector.tensor_scalar(m[:, 8, :], m[:, 8, :], -1.0, gn[:, 5:6], ALU.mult,
                                        ALU.add).then_inc(gn3a_done, b - a)

            def residual(b):
                s = slice(b * HW, (b + 1) * HW)
                dve.wait_ge(r3_done, b + 1)
                nc.vector.tensor_tensor(X[:, s], X[:, s], R3[:, b, :], ALU.add).then_inc(x1_done[b], 1)

            def token_stats(b):
                for i in range(PT):
                    if i % 2 == 0:
                        dve.wait_ge(tokc_done, (b * PT + i) // 2 + 1)
                    last = nc.vector.bn_stats(st4[:, b * PT + i, :], XTL[:, b * PT + i, 0:C])
                last.then_inc(tstat_done, 1)

            for b in range(3):
                channel_stats(b)
            channel_squares(0, 3)
            group_norm3(0, 3)
            residual(0)
            channel_stats(3)
            channel_squares(3, 4)
            residual(2)
            group_norm3(3, 4)
            token_stats(0)
            residual(3)
            token_stats(1)
            def te(v):
                return v.rearrange("p (t e) -> p t e", e=E)

            L, eq, code, oh1, oh2 = (te(g8[:, k, :]) for k in range(5))

            flat8 = g8.rearrange("p k n -> p (k n)")
            zeros, sl = g8[:, 5, :], g8[:, 0, :]
            before = flat8[:, 6 * E * TT:7 * E * TT + 1]

            def choose(a, b):
                n = b - a
                i8 = prm_("iota8").unsqueeze(1).to_broadcast([P, n, E])

                def wide(v):
                    return v[:, a:b].unsqueeze(2).to_broadcast([P, n, E])

                def largest(L, top, first, onehot):
                    chain(nc.vector.tensor_reduce(top[:, a:b], L, AX_X, ALU.max))
                    chain(nc.vector.tensor_tensor(eq[:, a:b, :], L, wide(top), ALU.is_equal))
                    chain(nc.vector.scalar_tensor_tensor(code[:, a:b, :], eq[:, a:b, :], -float(E), i8, ALU.mult, ALU.add))
                    chain(nc.vector.tensor_reduce(first[:, a:b], code[:, a:b, :], AX_X, ALU.min))
                    chain(nc.vector.tensor_tensor(onehot[:, a:b, :], code[:, a:b, :], wide(first), ALU.is_equal))

                dve.wait_ge(tokc_done, b // 2)
                raw = XTL[:, a:b, C:C + E]
                largest(raw, gw[:, 1, :], gw[:, 6, :], oh1)
                chain(nc.vector.scalar_tensor_tensor(L[:, a:b, :], oh1[:, a:b, :], -1e30, raw, ALU.mult, ALU.add))
                largest(L[:, a:b, :], gw[:, 5, :], gw[:, 6, :], oh2)

            nc.vector.memset(zeros, 0.0).then_inc(zeros_done, 1)
            nc.vector.memset(before[:, 0:1], 0.0).then_inc(zeros_done, 1)
            choose(0, 2 * PT)
            token_stats(2)
            choose(2 * PT, TT)
            et = "p (e t) -> p t e"
            nc.vector.tensor_tensor(mask16[:, :].rearrange(et, e=E), oh1, oh2, ALU.add).then_inc(mask_done, 1)
            nc.vector.tensor_tensor(gw[:, 2, :], gw[:, 5, :], gw[:, 1, :], ALU.subtract).then_inc(gsub_done, 1)
            token_stats(3)
            dve.wait_ge(rank_done, 1)
            dve.wait_ge(zeros_done, 2)
            chain(nc.vector.tensor_tensor_scan(before[:, 1:], bank(1, E * TT), zeros, 0.0, ALU.add, ALU.max))
            by_e = lambda v: v.rearrange("p (e t) -> p e t", e=E)
            begin, ends = by_e(before[:, :-1])[:, :, 0], by_e(before[:, 1:])[:, :, TT - 1]
            ntl, tend, off = (e8[:, k, :] for k in range(3))
            chain(nc.vector.scalar_tensor_tensor(e8i[:, 0, :], ends, float(P - 1), begin, ALU.add, ALU.subtract))
            chain(nc.vector.tensor_scalar(e8i[:, 1, :], e8i[:, 0, :], 7, None, ALU.arith_shift_right))
            chain(nc.vector.tensor_copy(ntl, e8i[:, 1, :]))
            chain(nc.vector.tensor_tensor_scan(tend, ntl, ntl, 0.0, ALU.add, ALU.max))
            chain(nc.vector.tensor_tensor(off, tend, ntl, ALU.subtract))
            chain(nc.vector.scalar_tensor_tensor(off, off, float(P), begin, ALU.mult, ALU.subtract))
            chain(nc.vector.tensor_tensor(sl, before[:, :-1], bank(0, E * TT), ALU.add))
            chain(nc.vector.tensor_tensor(by_e(sl), by_e(sl), off.unsqueeze(2).to_broadcast([P, E, TT]), ALU.add))
            for c, oh in enumerate((oh1, oh2)):
                chain(nc.vector.tensor_tensor(code, oh, sl.rearrange(et, e=E), ALU.mult))
                chain(nc.vector.tensor_reduce(slot[:, c * TT:(c + 1) * TT], code, AX_X, ALU.add))
            chain(nc.vector.tensor_copy(si[:, 0, :], slot[:, :]))
            chain(nc.vector.tensor_scalar(si[:, 1, :], si[:, 0, :], 7, None, ALU.arith_shift_right))
            nc.vector.tensor_scalar(si[:, 2, :], si[:, 0, :], P - 1, None, ALU.bitwise_and).then_inc(si_done, 1)
            nc.vector.tensor_copy(q16[:, :], si[:, 1, :]).then_inc(qr_done, 1)
            dve.wait_ge(si_done, 1)
            nc.vector.tensor_copy(r16[:, :], si[:, 2, :]).then_inc(qr_done, 1)
            dve.wait_ge(qr_done, 2)
            dve.wait_ge(wide_done, 1)
            for m in range(2 * TT // OHN):
                s = slice(m * OHN, (m + 1) * OHN)

                def over(v, k):
                    return v.unsqueeze(1).to_broadcast([P, k, OHN])

                nc.vector.tensor_tensor(OHQ[:, m, 2, :, :], IOTA_R[:, 0:NQ, :], over(q16[:, s], NQ),
                                        ALU.is_equal).then_inc(oh_done, 1)
                nc.vector.tensor_tensor(OHR[:, m, :, :], IOTA_R, over(r16[:, s], P), ALU.is_equal).then_inc(ohr_done, 1)
                dve.wait_ge(oh_done, m + 1)
                nc.vector.tensor_tensor(OHQ[:, m, 0, :, :], OHQ[:, m, 2, :, :], over(k16_("iota")[:, s], NQ),
                                        ALU.mult).then_inc(ohq_done, 1)
            gq = ge[:, :].rearrange("p (q e) -> p q e", e=E)
            chain(nc.vector.tensor_tensor(gq, prm_("iotaq").unsqueeze(2).to_broadcast([P, NQ, E]),
                                          tend.unsqueeze(1).to_broadcast([P, NQ, E]), ALU.is_ge))
            chain(nc.vector.tensor_reduce(eid[:, :], gq, AX_X, ALU.add))
            nc.vector.tensor_scalar(eidi[:, :], eid[:, :], float(E - 1), None, ALU.min).then_inc(eid_done, 1)
            dve.wait_ge(dest_done, 1)
            chain(nc.vector.tensor_copy(dst[:, 0, :], PS[:, 4, NQ:2 * NQ]))
            chain(nc.vector.scalar_tensor_tensor(dst[:, 1, :], bank(4, NQ), float(P), dst[:, 0, :], ALU.mult, ALU.add))
            chain(nc.vector.tensor_scalar(dsti[:, 0, :], dst[:, 1, :], -1.0, 0.0, ALU.add, ALU.max))
            chain(nc.vector.tensor_scalar(dsti[:, 1, :], dsti[:, 0, :], T - 1, None, ALU.bitwise_and))
            nc.vector.tensor_copy(gidx[:, 0:ILAG], dsti[:, 1, 0:ILAG]).then_inc(gidx_ready, ILAG)
            chain(nc.vector.tensor_scalar(dst[:, 0, :], dst[:, 1, :], 1.0, 4.0 * T, ALU.is_lt, ALU.mult))
            chain(nc.vector.scalar_tensor_tensor(dsti[:, 2, :], dst[:, 1, :], -1.0, dst[:, 0, :], ALU.add, ALU.add))

            for c, op in enumerate((ALU.is_le, ALU.is_gt)):
                nc.vector.tensor_scalar(chosen[:, c, :], dst[:, 1, :], float(T), None, op).then_inc(chosen_done, 1)

            def finish(q, slot, lap):
                dve.wait_ge(y_done, q + 1)
                at_least(dve, y_out[slot], 16 * lap)
                nc.vector.tensor_copy(sidx[:, slot:slot + 1], dsti[:, 2, bass.ds(q, 1)])
                nc.vector.tensor_tensor(gt[:, 0, slot:slot + 1], GX[:, slot, C:C + 1], chosen[:, 0, bass.ds(q, 1)],
                                        ALU.mult).then_inc(finish_step, 1)
                nc.vector.tensor_tensor(YH[:, slot % 4, :], PS[:, 4 + slot % 4, 0:C], part(slot, "b2"),
                                        ALU.add).then_inc(finish_step, 1)
                dve.wait_ge(finish_step, 3 * q + 1)
                nc.vector.scalar_tensor_tensor(gt[:, 1, slot:slot + 1], chosen[:, 1, bass.ds(q, 1)], GX[:, slot, C + 1:C + 2],
                                               gt[:, 0, slot:slot + 1], ALU.mult, ALU.add).then_inc(finish_step, 1)

            def next_index(q, slot, lap):
                at_least(dve, g_in[slot], 16 * lap)
                nc.vector.tensor_copy(gidx[:, slot:slot + 1], dsti[:, 1, bass.ds(q, 1)]).then_inc(gidx_ready, 1)

            def take_expert(q, slot, lap):
                at_least(dve, finish_step, 3 * (q - 3))
                e = nc.values_load(eidi[0:1, bass.ds(q, 1)], engines=(mybir.EngineType.DVE,), min_val=0, max_val=E - 1,
                                   skip_runtime_bounds_check_because="a minimum with E - 1 bounds it")
                nc.vector.tensor_copy(WE[:, slot % 4, :], WALL[:, bass.ds(e, 1), :].rearrange("p e n -> p (e n)")).then_inc(we_ready, 1)

            for w in range(2):
                dve.wait_ge(w_in[w], 16)
            dve.wait_ge(eid_done, 1)
            dve.wait_ge(chosen_done, 2)
            for b in range(B):
                dve.wait_ge(rows_out[b], 16)
            for q in range(WLEAD):
                take_expert(*tile(0, q))

            def step(i, j):
                if exists(tile(i, j, WLEAD)[0]):
                    take_expert(*tile(i, j, WLEAD))
                if exists(tile(i, j, ILAG)[0]):
                    next_index(*tile(i, j, ILAG))
                if exists(tile(i, j, -OLAG)[0]):
                    finish(*tile(i, j, -OLAG))

            run_steps(dve, step)
            for b in range(B + 1):
                if b < B:
                    if b >= 2:
                        dve.wait_ge(ot_done, 2 * (b - 1))
                    for h in range(2):
                        dve.wait_ge(y_in[2 * b + h], 32)
                        s = slice(b * PT + h * PT // 2, b * PT + (h + 1) * PT // 2)
                        nc.vector.tensor_tensor(CMB[:, b % 2, h * PT // 2:(h + 1) * PT // 2, :], YIN[:, 0, s, :],
                                                YIN[:, 1, s, :], ALU.add).then_inc(comb_done, 1)
                if b >= 1:
                    c = b - 1
                    if c >= 2:
                        dve.wait_ge(out_done[c - 2], 32)
                    for h in range(2):
                        dve.wait_ge(ot_done, 2 * c + h + 1)
                        nc.vector.tensor_tensor(OUT[:, c % 2, h * HALF:(h + 1) * HALF], bank(2 * (c % 2) + h),
                                                X[:, c * HW + h * HALF:c * HW + (h + 1) * HALF], ALU.add).then_inc(fin_done, 1)

        @block.tensor
        def _(pe):
            pe.wait_ge(small_in, 16)
            nc.tensor.matmul(bank(7, CI + E), prm_("avg"), prm[:, COLS["w1"][0]:COLS["gate"][1]],
                             start=True, stop=True).then_inc(wmean_done, 1)

            def per_image(first_bank, lhs, rhs, done, wait=None):
                for h in range(2):
                    for b in range(B):
                        if wait:
                            wait(b)
                        last = nc.tensor.matmul(PS[b * CI:(b + 1) * CI, first_bank + h, :], lhs,
                                                rhs[:, b * HW + h * HALF:b * HW + (h + 1) * HALF], start=True, stop=True)
                    last.then_inc(done, 1)

            per_image(0, prm_("avg")[:, 0:CI], X, mean_done, lambda b: pe.wait_ge(x_in[b], 16))
            per_image(4, prm_("avg")[:, 0:CI], XSQ, msq_done, lambda b: pe.wait_ge(xsq_done, b + 1))
            pe.wait_ge(wc_ready, 1)
            per_image(2, WC1[:, :], X, u_done)

            def keep_busy(n, b):
                for _ in range(n):
                    nc.tensor.matmul(bank(b), k16_("ident"), k16_("sel")[:, 0:HALF], start=True, stop=True)

            def logits(d, tap):
                if tap == 0 and d >= 1:
                    pe.wait_ge(log_done, 2 * d)
                for h in range(2):
                    for i, t in enumerate(XP):
                        if d == 0 and tap == 0 and h == 0:
                            pe.wait_ge(xl_done, i + 1)
                        last = nc.tensor.matmul(PS[i * (P // 2):(i + 1) * (P // 2), h, :], WCB[:, tap, d, :],
                                                tap_view(t, DILS[d], tap, h * RH, RH), start=(tap == 0), stop=(tap == KK - 1))
                if tap == KK - 1:
                    last.then_inc(logit_done, 1)

            def turn_logits(d, i):
                if i % (PT // 2) == 0:
                    pe.wait_ge(log_done, 2 * d + 1 + (i > 0))
                    if d >= 1:
                        pe.wait_ge(ftc_done, d)
                last = nc.tensor.matmul(PS[:, 5, i * B * KK:(i + 1) * B * KK], LOG[:, d % 2, i * P:(i + 1) * P],
                                        prm_("fold"), start=True, stop=True)
                if i == PT - 1:
                    last.then_inc(tlog_done, 1)

            def turn_filters(d):
                pe.wait_ge(fhl_done, d + 1)
                w = 2 * B * KK
                for i in range(PT):
                    last = nc.tensor.transpose(PS[0:w, 5, i * (P // 2):(i + 1) * (P // 2)].bitcast(F16),
                                               FHL[:, d, :, :].rearrange("p a b -> p (a b)")[:, i * w:(i + 1) * w],
                                               k16_("ident"))
                last.then_inc(ft_done, 1)

            def spread(g):
                n, h = g // 2, g % 2
                d, k = n // KK, n % KK
                if k == 0 and h == 0:
                    pe.wait_ge(ftc_done, d + 1)
                if g >= 3:
                    pe.wait_ge(prod_done, g - 2)
                nc.tensor.matmul(bank(FB_BANK[g % 3]), k16_("sel")[0:8 * KK, k * P:(k + 1) * P],
                                 FT[0:8 * KK, d, h * HALF:(h + 1) * HALF], start=True, stop=True).then_inc(fb_done, 1)

            def accumulate(d, what, h):
                if what == "S":
                    pe.wait_ge(ring_used, of_kind("s", (d + 1) * KK))
                    source = SUM2[:, d % 2, :]
                elif what == "D":
                    pe.wait_ge(own_used, d + 1)
                    source = SUM1[:, d % 2, :]
                else:
                    pe.wait_ge(prod_done, 2 * what + h + 1)
                    source = product_buffer(what)
                nc.tensor.matmul(bank(6 + h), W2B[:, 1 + d, :], source[:, h * HALF:(h + 1) * HALF], start=False,
                                 stop=(d, what, h) == [a[1:] for a in ACCUMULATE if a[3] == h][-1]).then_inc(acc_done, 1)

            pe.wait_ge(c16_in, 16)
            keep_busy(30, 6)
            pe.wait_ge(wcb_ready, 2 * B)
            for tap in range(KK):
                logits(0, tap)
            pe.wait_ge(w2b_ready, 2 * B)
            pe.wait_ge(xd_done, 1)
            for h in range(2):
                last = nc.tensor.matmul(bank(6 + h), W2B[:, 0, :], tap_view(XD, 1, KK // 2, h * RH, RH),
                                        start=True, stop=False)
            last.then_inc(acc_done, 1)
            for i in range(PT):
                turn_logits(0, i)
            for tap in range(KK):
                logits(1, tap)
                if tap == FIRST_FILTERS_AFTER:
                    turn_filters(0)
            for g in range(ACCUMULATE[-1][0] + 1):
                if g < 2 * NPR:
                    spread(g)
                for at, d, what, h in ACCUMULATE:
                    if at == g:
                        accumulate(d, what, h)
                d, at = divmod(g, 2 * KK)
                if d + 1 < ND and at < PT:
                    turn_logits(d + 1, at)
                if d + 1 < ND and at == FILTERS_AT:
                    turn_filters(d + 1)
                for tap in range(KK):
                    if d + 2 < ND and LOGITS_AT[tap] == at:
                        logits(d + 2, tap)

            keep_busy(12, 5)

            def third_conv(b):
                if b == 0:
                    pe.wait_ge(w3z_ready, B)
                    pe.wait_ge(y2_done, 1)
                    pe.wait_ge(prod_done, 2 * NPR)
                if b == 3:
                    pe.wait_ge(r3_done, 1)
                for h in range(2):
                    last = nc.tensor.matmul(bank(Y3_BANK[b] + h), W3Z[:, b, :], Y2[:, h * HALF:(h + 1) * HALF],
                                            start=True, stop=True)
                last.then_inc(y3_done, 1)

            def group_means(a, b):
                pe.wait_ge(gs_done, b)
                nc.tensor.matmul(bank(4, 2 * (b - a)), prm_("group"), mv3[:, 0:2, a:b],
                                 start=True, stop=True).then_inc(gm_done, b - a)

            def tokens(b):
                pe.wait_ge(x1_done[b], 1)
                for g in range(b * PT // 2, (b + 1) * PT // 2):
                    if g == 1:
                        pe.wait_ge(r3_done, 2)
                    if g >= 3:
                        pe.wait_ge(tokc_done, g - 2)
                    for i in range(2):
                        t = 2 * g + i
                        last = nc.tensor.matmul(PS[:, TOKEN_BANK[g % 3], i * (C + E):(i + 1) * (C + E)],
                                                X[:, t * P:(t + 1) * P], RG[:, :], start=True, stop=True)
                    last.then_inc(tok_done, 1)

            for b in range(3):
                third_conv(b)
            keep_busy(10, 5)
            group_means(0, 3)
            keep_busy(12, 5)
            third_conv(3)
            tokens(0)
            group_means(3, 4)
            for b in range(1, B):
                tokens(b)
            pe.wait_ge(mask_done, 1)
            nc.tensor.matmul(bank(0, E * TT), k16_("before"), mask16[:, :], start=True, stop=True)
            nc.tensor.matmul(bank(1, E * TT), k16_("ones"), mask16[:, :], start=True, stop=True).then_inc(rank_done, 1)
            for n in range(2 * TT):
                m = n // OHN
                if n % OHN == 0:
                    for ready in (ohp_done, ohr_done, ohq_done):
                        pe.wait_ge(ready, m + 1)
                last = nc.tensor.matmul(bank(4, 2 * NQ), OHR[:, m, :, n % OHN], OHQ[:, m, 0:2, :, n % OHN],
                                        start=(n == 0), stop=(n == 2 * TT - 1))
            last.then_inc(dest_done, 1)
            keep_busy(16, 7)

            def turn(q, slot, lap):
                pe.wait_ge(g_in[slot], 16 * (lap + 1))
                last = nc.tensor.transpose(PS[:, slot % 2, 0:P], GX[:, slot, 0:C], prm_("ident"))
                last.then_inc(xt_done, 1)

            def hidden(q, slot, lap):
                pe.wait_ge(we_ready, q + 1)
                pe.wait_ge(xtc_done, q + 1)
                for c in range(HC):
                    last = nc.tensor.matmul(PS[:, 2 + slot % 2, c * P:(c + 1) * P], part(slot, "w1")[:, c * P:(c + 1) * P],
                                            XT[:, slot % 4, :], start=True, stop=True)
                last.then_inc(h_done, 1)

            def output(q, slot, lap):
                pe.wait_ge(gelu_done, q + 1)
                for c in range(HC):
                    last = nc.tensor.matmul(PS[:, 4 + slot % 4, 0:C], GF[:, slot % 2, c * P:(c + 1) * P],
                                            part(slot, "w2")[:, c * C:(c + 1) * C], start=(c == 0), stop=(c == HC - 1))
                last.then_inc(y_done, 1)

            for q in range(TLEAD):
                turn(*tile(0, q))

            def step(i, j):
                if exists(tile(i, j)[0]):
                    hidden(*tile(i, j))
                if exists(tile(i, j, TLEAD)[0]):
                    turn(*tile(i, j, TLEAD))
                if exists(tile(i, j, -OLAG)[0]):
                    output(*tile(i, j, -OLAG))

            run_steps(pe, step)
            for b in range(B):
                if b >= 2:
                    pe.wait_ge(fin_done, 2 * (b - 1))
                for h in range(2):
                    pe.wait_ge(comb_done, 2 * b + h + 1)
                    for i in range(PT // 2):
                        last = nc.tensor.transpose(PS[:, 2 * (b % 2) + h, i * P:(i + 1) * P],
                                                   CMB[:, b % 2, h * PT // 2 + i, :], prm_("ident"))
                    last.then_inc(ot_done, 1)


def kernel(**inputs):
    import concourse.bacc as _bacc
    from concourse.bass_utils import run_bass_kernel_spmd as _run

    a = {k.replace("L0_", ""): np.asarray(v) for k, v in inputs.items()}
    rep = lambda v: np.tile(v, (B, 1))
    col = lambda v, n: np.tile(v.reshape(-1, 1), (n, 1))
    wcat = np.stack([a[f"conv_w_cat{s}"].reshape(KK, CI, KK).transpose(1, 2, 0) for s in "abcd"], 2)
    c32, c16 = shape_constants()
    small = np.concatenate([
        col(a["conv_gn1_g"], B), col(a["conv_gn1_b"], B), col(a["conv_gn2_g"], B), col(a["conv_gn2_b"], B),
        col(a["conv_gn3_g"], 1), col(a["conv_gn3_b"], 1),
        a["conv_w_scale1"].reshape(CI, C).T, a["ffn_gate_w"].T,
        rep(wcat.reshape(CI, -1)),
        rep(a["conv_w_scale2"].reshape(CI, 5, CI).transpose(2, 1, 0).reshape(CI, -1)),
        rep(a["conv_w_scale3"].reshape(C, CI).T),
        c32], 1)
    arrays = {
        "x": a["x"].reshape(B, C, HW), "small": small, "c16": c16,
        "experts": np.concatenate([
            a["ffn_w1"].transpose(2, 0, 1),
            a["ffn_w2"].reshape(E, C, HC, P).transpose(3, 0, 2, 1).reshape(P, E, HID),
            a["ffn_b1"].reshape(E, HC, P).transpose(2, 0, 1),
            np.tile(a["ffn_b2"].reshape(1, E, C), (P, 1, 1))], 2),
    }
    arrays = {k: np.ascontiguousarray(v) for k, v in arrays.items()}
    nc = _bacc.Bacc("TRN2", target_bir_lowering=False, num_devices=1)
    aps = {k: nc.dram_tensor(k, v.shape, mybir.dt.from_np(v.dtype), kind="ExternalInput").ap() for k, v in arrays.items()}
    out = nc.dram_tensor("out", [B, C, HW], F32, kind="ExternalOutput").ap()
    build(nc, out=out, **aps)
    r = _run(nc, [arrays], core_ids=[0])
    return r.results[0]["out"].reshape(B, C, HH, WW)
```
